# Optimizing a Trainium2 kernel written in Bass

```python
import numpy as np
import jax
import jax.numpy as jnp

def _softmax(x, axis=-1):
    return jax.nn.softmax(x, axis=axis)

def _gelu(x):
    return jax.nn.gelu(x, approximate=True)

def _silu(x):
    return jax.nn.silu(x)

def _sigmoid(x):
    return jax.nn.sigmoid(x)

def _layernorm(x, axis=-1, eps=1e-05):
    m = jnp.mean(x, axis=axis, keepdims=True)
    v = jnp.var(x, axis=axis, keepdims=True)
    return (x - m) / jnp.sqrt(v + eps)

def _scatter_add(tgt, idx, src, axis=0):
    return tgt.at[idx].add(src)

def _segment_sum(src, seg, n):
    return jax.ops.segment_sum(src, seg, n)
kernel_name = 'mk_gnn_preln_d4_gnn_r32_a0ab8e'

def setup_inputs(seed: int=0):
    np.random.seed(seed)
    _w = jnp.asarray

    def _rec_inputs():
        import jax
        import jax.numpy as jnp
        _gk = jax.random.key(seed)
        x = -8.776e-05 + 1 * jax.random.normal(jax.random.fold_in(_gk, 1), (3125, 128), jnp.float32)
        _s = jax.random.randint(jax.random.fold_in(_gk, 2), (25000,), 0, 3125, jnp.int32)
        _d = jax.random.randint(jax.random.fold_in(_gk, 3), (25000,), 0, 3125, jnp.int32)
        _loop = jnp.arange(3125, dtype=jnp.int32)
        src = jnp.concatenate([_s, _d, _loop])
        dst = jnp.concatenate([_d, _s, _loop])
        _o = jnp.argsort(dst, stable=True)
        src = src[_o]
        dst = dst[_o]
        edge_attr_128 = -8.16379e-05 + 0.999858 * jax.random.normal(jax.random.fold_in(_gk, 12), (53125, 128), jnp.float32)
        edge_weight = jax.random.uniform(jax.random.fold_in(_gk, 14), (53125,), jnp.float32, 0.0, 12)
        return (x, src, dst, edge_attr_128, edge_weight)
    x, src, dst, edge_attr_128, edge_weight = _rec_inputs()

    def _L0_gnn_setup():
        import jax, jax.numpy as jnp
        import numpy as np
        import math
        N_ATOMS = 1250
        HIDDEN = 128
        NUM_RBF = 50
        CUTOFF = 10.0
        N_EDGES = 20000
        key = jax.random.key(seed)
        ks = jax.random.split(key, 12)
        s = lambda fan_in: 1.0 / np.sqrt(fan_in)
        inp = {'h': jax.random.normal(ks[0], (N_ATOMS, HIDDEN), dtype=jnp.float32), 'edge_index': jax.random.randint(ks[1], (2, N_EDGES), 0, N_ATOMS, dtype=jnp.int64), 'distances': jax.random.uniform(ks[2], (N_EDGES,), dtype=jnp.float32) * 12.0, 'fw1': jax.random.uniform(ks[3], (NUM_RBF, HIDDEN), jnp.float32, -s(NUM_RBF), s(NUM_RBF)), 'fb1': jnp.zeros((HIDDEN,), jnp.float32), 'fw2': jax.random.uniform(ks[4], (HIDDEN, HIDDEN), jnp.float32, -s(HIDDEN), s(HIDDEN)), 'fb2': jnp.zeros((HIDDEN,), jnp.float32), 'pw': jax.random.uniform(ks[5], (HIDDEN, HIDDEN), jnp.float32, -s(HIDDEN), s(HIDDEN)), 'pb': jnp.zeros((HIDDEN,), jnp.float32), 'mw1': jax.random.uniform(ks[6], (HIDDEN, HIDDEN), jnp.float32, -s(HIDDEN), s(HIDDEN)), 'mb1': jnp.zeros((HIDDEN,), jnp.float32), 'mw2': jax.random.uniform(ks[7], (HIDDEN, HIDDEN), jnp.float32, -s(HIDDEN), s(HIDDEN)), 'mb2': jnp.zeros((HIDDEN,), jnp.float32)}
        return inp
    _L0_gnn_all = _L0_gnn_setup()
    _L0_gnn_in = {k: v for k, v in _L0_gnn_all.items() if k in ('fw1', 'fb1', 'fw2', 'fb2', 'pw', 'pb', 'mw1', 'mb1', 'mw2', 'mb2')}
    del _L0_gnn_all

    def _L1_gnn_setup():
        import jax, jax.numpy as jnp
        import numpy as np
        N_NODES = 50000
        N_EDGES = 25000
        IN_FEATS = 128
        OUT_FEATS = 128
        key = jax.random.key(seed)
        k1, k2, k3, k4, k5 = jax.random.split(key, 5)
        feature = jax.random.normal(k1, (N_NODES, IN_FEATS), dtype=jnp.float32)
        src = jax.random.randint(k2, (N_EDGES,), 0, N_NODES, dtype=jnp.int64)
        dst = jax.random.randint(k3, (N_EDGES,), 0, N_NODES, dtype=jnp.int64)
        lim = 1.0 / np.sqrt(IN_FEATS)
        W = jax.random.uniform(k4, (IN_FEATS, OUT_FEATS), dtype=jnp.float32, minval=-lim, maxval=lim)
        b = jax.random.uniform(k5, (OUT_FEATS,), dtype=jnp.float32, minval=-lim, maxval=lim)
        return {'feature': feature, 'src': src, 'dst': dst, 'W': W, 'b': b}
    _L1_gnn_all = _L1_gnn_setup()
    _L1_gnn_in = {k: v for k, v in _L1_gnn_all.items() if k in ('W', 'b')}
    del _L1_gnn_all

    def _L2_gnn_setup():
        import jax, jax.numpy as jnp
        import numpy as np
        LN_EPS = 1e-05
        N, E, D = (50000, 25000, 128)
        H = 4 * D
        key = jax.random.key(seed)
        ks = jax.random.split(key, 8)
        h = jax.random.normal(ks[0], (N, D), dtype=jnp.float32)
        e_ij = jax.random.normal(ks[1], (E, D), dtype=jnp.float32)
        src = jax.random.randint(ks[2], (E,), 0, N, dtype=jnp.int32)
        dst = jax.random.randint(ks[3], (E,), 0, N, dtype=jnp.int32)
        W1 = jax.random.normal(ks[4], (D, H), dtype=jnp.float32) / np.sqrt(D)
        b1 = jnp.zeros((H,), dtype=jnp.float32)
        W2 = jax.random.normal(ks[5], (H, D), dtype=jnp.float32) / np.sqrt(H)
        b2 = jnp.zeros((D,), dtype=jnp.float32)
        gamma = jnp.ones((D,), dtype=jnp.float32)
        beta = jnp.zeros((D,), dtype=jnp.float32)
        return {'h': h, 'e_ij': e_ij, 'src': src, 'dst': dst, 'W1': W1, 'b1': b1, 'W2': W2, 'b2': b2, 'gamma': gamma, 'beta': beta}
    _L2_gnn_all = _L2_gnn_setup()
    _L2_gnn_in = {k: v for k, v in _L2_gnn_all.items() if k in ('W1', 'b1', 'W2', 'b2', 'gamma', 'beta')}
    del _L2_gnn_all

    def _L3_gnn_setup():
        import jax, jax.numpy as jnp
        import numpy as np
        N_NODES = 625
        N_EDGES = 8000
        DIM = 128
        N_LAYERS = 4

        def _bn(x, gamma, beta, eps=1e-05):
            mu = x.mean(0)
            var = ((x - mu) ** 2).mean(0)
            return gamma * (x - mu) * jax.lax.rsqrt(var + eps) + beta
        key = jax.random.key(seed)
        ks = jax.random.split(key, 32)
        s = 1.0 / np.sqrt(DIM)
        inp = {'h': jax.random.normal(ks[0], (N_NODES, DIM), jnp.float32), 'e': jax.random.normal(ks[1], (N_EDGES, DIM), jnp.float32), 'src': jax.random.randint(ks[2], (N_EDGES,), 0, N_NODES, jnp.int32), 'dst': jax.random.randint(ks[3], (N_EDGES,), 0, N_NODES, jnp.int32), 'W_emb_h': jax.random.normal(ks[4], (DIM, DIM), jnp.float32) * s, 'b_emb_h': jnp.zeros((DIM,), jnp.float32), 'W_emb_e': jax.random.normal(ks[5], (DIM, DIM), jnp.float32) * s, 'b_emb_e': jnp.zeros((DIM,), jnp.float32)}
        for i, nm in enumerate(['A', 'B', 'C', 'D', 'E']):
            inp[nm + 'w'] = jax.random.normal(ks[6 + i], (N_LAYERS, DIM, DIM), jnp.float32) * s
            inp[nm + 'b'] = jnp.zeros((N_LAYERS, DIM), jnp.float32)
        inp['gh'] = jnp.ones((N_LAYERS, DIM), jnp.float32)
        inp['bh'] = jnp.zeros((N_LAYERS, DIM), jnp.float32)
        inp['ge'] = jnp.ones((N_LAYERS, DIM), jnp.float32)
        inp['be'] = jnp.zeros((N_LAYERS, DIM), jnp.float32)
        return inp
    _L3_gnn_all = _L3_gnn_setup()
    _L3_gnn_in = {k: v for k, v in _L3_gnn_all.items() if k in ('W_emb_h', 'b_emb_h', 'W_emb_e', 'b_emb_e', 'Aw', 'Ab', 'Bw', 'Bb', 'Cw', 'Cb', 'Dw', 'Db', 'Ew', 'Eb', 'gh', 'bh', 'ge', 'be')}
    del _L3_gnn_all
    return {'x': x, 'src': src, 'dst': dst, 'edge_attr_128': edge_attr_128, 'edge_weight': edge_weight, 'L0_gnn_fw1': _L0_gnn_in['fw1'], 'L0_gnn_fb1': _L0_gnn_in['fb1'], 'L0_gnn_fw2': _L0_gnn_in['fw2'], 'L0_gnn_fb2': _L0_gnn_in['fb2'], 'L0_gnn_pw': _L0_gnn_in['pw'], 'L0_gnn_pb': _L0_gnn_in['pb'], 'L0_gnn_mw1': _L0_gnn_in['mw1'], 'L0_gnn_mb1': _L0_gnn_in['mb1'], 'L0_gnn_mw2': _L0_gnn_in['mw2'], 'L0_gnn_mb2': _L0_gnn_in['mb2'], 'L1_gnn_W': _L1_gnn_in['W'], 'L1_gnn_b': _L1_gnn_in['b'], 'L2_gnn_W1': _L2_gnn_in['W1'], 'L2_gnn_b1': _L2_gnn_in['b1'], 'L2_gnn_W2': _L2_gnn_in['W2'], 'L2_gnn_b2': _L2_gnn_in['b2'], 'L2_gnn_gamma': _L2_gnn_in['gamma'], 'L2_gnn_beta': _L2_gnn_in['beta'], 'L3_gnn_W_emb_h': _L3_gnn_in['W_emb_h'], 'L3_gnn_b_emb_h': _L3_gnn_in['b_emb_h'], 'L3_gnn_W_emb_e': _L3_gnn_in['W_emb_e'], 'L3_gnn_b_emb_e': _L3_gnn_in['b_emb_e'], 'L3_gnn_Aw': _L3_gnn_in['Aw'], 'L3_gnn_Ab': _L3_gnn_in['Ab'], 'L3_gnn_Bw': _L3_gnn_in['Bw'], 'L3_gnn_Bb': _L3_gnn_in['Bb'], 'L3_gnn_Cw': _L3_gnn_in['Cw'], 'L3_gnn_Cb': _L3_gnn_in['Cb'], 'L3_gnn_Dw': _L3_gnn_in['Dw'], 'L3_gnn_Db': _L3_gnn_in['Db'], 'L3_gnn_Ew': _L3_gnn_in['Ew'], 'L3_gnn_Eb': _L3_gnn_in['Eb'], 'L3_gnn_gh': _L3_gnn_in['gh'], 'L3_gnn_bh': _L3_gnn_in['bh'], 'L3_gnn_ge': _L3_gnn_in['ge'], 'L3_gnn_be': _L3_gnn_in['be']}

def reference(x, src, dst, edge_attr_128, edge_weight, L0_gnn_fw1, L0_gnn_fb1, L0_gnn_fw2, L0_gnn_fb2, L0_gnn_pw, L0_gnn_pb, L0_gnn_mw1, L0_gnn_mb1, L0_gnn_mw2, L0_gnn_mb2, L1_gnn_W, L1_gnn_b, L2_gnn_W1, L2_gnn_b1, L2_gnn_W2, L2_gnn_b2, L2_gnn_gamma, L2_gnn_beta, L3_gnn_W_emb_h, L3_gnn_b_emb_h, L3_gnn_W_emb_e, L3_gnn_b_emb_e, L3_gnn_Aw, L3_gnn_Ab, L3_gnn_Bw, L3_gnn_Bb, L3_gnn_Cw, L3_gnn_Cb, L3_gnn_Dw, L3_gnn_Db, L3_gnn_Ew, L3_gnn_Eb, L3_gnn_gh, L3_gnn_bh, L3_gnn_ge, L3_gnn_be):
    import jax
    import jax.numpy as jnp

    def _L0_gnn_ref(h, edge_index, distances, fw1, fb1, fw2, fb2, pw, pb, mw1, mb1, mw2, mb2):
        import jax, jax.numpy as jnp
        import numpy as np
        import math
        N_ATOMS = 1250
        HIDDEN = 128
        NUM_RBF = 50
        CUTOFF = 10.0
        N_EDGES = 20000
        src, dst = (edge_index[0], edge_index[1])
        num_atoms = h.shape[0]
        width = CUTOFF / NUM_RBF * 0.5
        centers = jnp.linspace(0.0, CUTOFF, NUM_RBF)
        rbf = jnp.exp(-(distances[:, None] - centers) ** 2 / (2.0 * width * width))
        cut = 0.5 * (jnp.cos(jnp.pi * distances / CUTOFF) + 1.0) * (distances <= CUTOFF).astype(h.dtype)
        W = (jax.nn.silu(rbf @ fw1 + fb1) @ fw2 + fb2) * cut[:, None]
        messages = (h[src] @ pw + pb) * W
        agg = jax.ops.segment_sum(messages, dst, num_segments=num_atoms)
        return h + (jax.nn.silu(agg @ mw1 + mb1) @ mw2 + mb2)

    def _L1_gnn_ref(feature, src, dst, W, b):
        import jax, jax.numpy as jnp
        import numpy as np
        N_NODES = 50000
        N_EDGES = 25000
        IN_FEATS = 128
        OUT_FEATS = 128
        n = feature.shape[0]
        msg_sum = jax.ops.segment_sum(feature[src], dst, num_segments=n)
        deg = jax.ops.segment_sum(jnp.ones((src.shape[0],), feature.dtype), dst, num_segments=n)
        deg_safe = jnp.maximum(deg, 1.0)
        mean = msg_sum / deg_safe[:, None]
        h = jnp.where((deg > 0)[:, None], mean, feature)
        return jax.nn.relu(h @ W + b)

    def _L2_gnn_ref(h, e_ij, src, dst, W1, b1, W2, b2, gamma, beta):
        import jax, jax.numpy as jnp
        import numpy as np
        LN_EPS = 1e-05
        N = h.shape[0]
        neigh = jax.ops.segment_sum(h[src], dst, num_segments=N)
        u_edge = jax.ops.segment_sum(e_ij, dst, num_segments=N)
        u = neigh + u_edge
        hid = jax.nn.relu(u @ W1 + b1)
        out = hid @ W2 + b2 + h
        mean = jnp.mean(out, axis=-1, keepdims=True)
        var = jnp.var(out, axis=-1, keepdims=True)
        normed = (out - mean) * jax.lax.rsqrt(var + LN_EPS)
        return normed * gamma + beta

    def _L3_gnn_ref(h, e, src, dst, W_emb_h, b_emb_h, W_emb_e, b_emb_e, Aw, Ab, Bw, Bb, Cw, Cb, Dw, Db, Ew, Eb, gh, bh, ge, be):
        import jax, jax.numpy as jnp
        import numpy as np
        N_NODES = 625
        N_EDGES = 8000
        DIM = 128
        N_LAYERS = 4

        def _bn(x, gamma, beta, eps=1e-05):
            mu = x.mean(0)
            var = ((x - mu) ** 2).mean(0)
            return gamma * (x - mu) * jax.lax.rsqrt(var + eps) + beta
        n_nodes = h.shape[0]
        h = h @ W_emb_h + b_emb_h
        e = e @ W_emb_e + b_emb_e
        for l in range(Aw.shape[0]):
            h_in, e_in = (h, e)
            Ah = h @ Aw[l] + Ab[l]
            Bh = h @ Bw[l] + Bb[l]
            Dh = h @ Dw[l] + Db[l]
            Eh = h @ Ew[l] + Eb[l]
            Ce = e @ Cw[l] + Cb[l]
            e_new = Dh[src] + Eh[dst] + Ce
            sigma = jax.nn.sigmoid(e_new)
            num = jax.ops.segment_sum(sigma * Bh[src], dst, num_segments=n_nodes)
            den = jax.ops.segment_sum(sigma, dst, num_segments=n_nodes)
            h_new = Ah + num / (den + 1e-06)
            h_new = _bn(h_new, gh[l], bh[l])
            e_new = _bn(e_new, ge[l], be[l])
            h = h_in + jax.nn.relu(h_new)
            e = e_in + jax.nn.relu(e_new)
        return h
    edge_index = jnp.stack([src, dst])
    h = jnp.maximum(_layernorm(x, axis=-1), 0.0)
    x = x + _L0_gnn_ref(h, edge_index, edge_weight, L0_gnn_fw1, L0_gnn_fb1, L0_gnn_fw2, L0_gnn_fb2, L0_gnn_pw, L0_gnn_pb, L0_gnn_mw1, L0_gnn_mb1, L0_gnn_mw2, L0_gnn_mb2)
    h = jnp.maximum(_layernorm(x, axis=-1), 0.0)
    x = x + _L1_gnn_ref(h, src, dst, L1_gnn_W, L1_gnn_b)
    h = jnp.maximum(_layernorm(x, axis=-1), 0.0)
    x = x + _L2_gnn_ref(h, edge_attr_128, src, dst, L2_gnn_W1, L2_gnn_b1, L2_gnn_W2, L2_gnn_b2, L2_gnn_gamma, L2_gnn_beta)
    h = jnp.maximum(_layernorm(x, axis=-1), 0.0)
    x = x + _L3_gnn_ref(h, edge_attr_128, src, dst, L3_gnn_W_emb_h, L3_gnn_b_emb_h, L3_gnn_W_emb_e, L3_gnn_b_emb_e, L3_gnn_Aw, L3_gnn_Ab, L3_gnn_Bw, L3_gnn_Bb, L3_gnn_Cw, L3_gnn_Cb, L3_gnn_Dw, L3_gnn_Db, L3_gnn_Ew, L3_gnn_Eb, L3_gnn_gh, L3_gnn_bh, L3_gnn_ge, L3_gnn_be)
    return x

_drawn_inputs = setup_inputs


def setup_inputs(seed=0):
    import zlib

    import numpy as np

    out = dict(_drawn_inputs(seed))
    spreads = {'L0_gnn_fb1': (0.0, 0.8),
     'L0_gnn_fb2': (0.0, 0.507),
     'L0_gnn_pb': (0.0, 0.8),
     'L0_gnn_mb1': (0.0, 0.559),
     'L0_gnn_mb2': (0.0, 0.287),
     'L2_gnn_b1': (0.0, 2.0),
     'L2_gnn_b2': (0.0, 2.0),
     'L2_gnn_gamma': (1.0, 0.2),
     'L2_gnn_beta': (0.0, 0.324),
     'L3_gnn_b_emb_h': (0.0, 0.389),
     'L3_gnn_b_emb_e': (0.0, 2.0),
     'L3_gnn_Ab': (0.0, 2.0),
     'L3_gnn_Bb': (0.0, 2.0),
     'L3_gnn_Cb': (0.0, 2.0),
     'L3_gnn_Db': (0.0, 2.0),
     'L3_gnn_Eb': (0.0, 2.0),
     'L3_gnn_gh': (1.0, 0.2),
     'L3_gnn_bh': (0.0, 0.1),
     'L3_gnn_ge': (1.0, 0.6),
     'L3_gnn_be': (0.0, 2.0)}
    factors = {'edge_weight': 8.0,
     'L0_gnn_fw1': 8.0,
     'L0_gnn_fw2': 8.0,
     'L0_gnn_pw': 3.189,
     'L0_gnn_mw1': 3.925,
     'L1_gnn_b': 3.571}
    for name, (base, spread) in spreads.items():
        noise = np.random.default_rng([zlib.crc32(name.encode()), seed]).standard_normal(out[name].shape)
        drawn = base * np.exp(spread * noise) if base else spread * noise
        out[name] = jnp.asarray(drawn.astype(out[name].dtype))
    for name, factor in factors.items():
        out[name] = (out[name] * factor).astype(out[name].dtype)
    return out
```

```python
from contextlib import ExitStack

import numpy as np
import concourse.bass as bass
from concourse import mybir
from concourse.alu_op_type import AluOpType as ALU

F32 = mybir.dt.float32
I32 = mybir.dt.int32
ACT = mybir.ActivationFunctionType
AX_X = mybir.AxisListType.X

P = 128
N = 3125
W = 64
NW = -(-N // W)
NP = NW * W
NCH = 7
CH = NP // NCH
LAST = N - (NCH - 1) * CH
NT = -(-NP // P)
E = 53125
T = 4
GE = T * P
G = -(-E // GE)
EP = G * GE
ELAST = E - (G - 1) * GE
U = 4
R = G // U
FIRST_SEM = 128
RBF = 50
CUTOFF = 10.0
WIDTH = CUTOFF / RBF * 0.5
LAYERS = 4
LN_EPS = 1e-5
BN_EPS = 1e-5
assert G % U == 0 and NP % NCH == 0 and CH <= 512

MATS = {"fw2": 0, "pw": 1, "mw1": 2, "mw2": 3, "L1": 4, "W1": 5, "W2": 9, "emb_h": 13, "emb_e": 14}
LAYER_MATS = 15
NMATS = LAYER_MATS + 5 * LAYERS
COLS = {"fb1": 0, "mb1": 1, "mb2": 2, "L1": 3, "b1": 4, "b2": 8, "gamma": 9, "beta": 10, "emb_h": 11,
        "emb_e": 12, "half_fb1": 13, "half_mb1": 14}
LAYER_COLS = 15
NCOLS = LAYER_COLS + 5 * LAYERS
ROWS = {"pb": 0, "fb2": 1}
LAYER_ROWS = 2
NROWS = LAYER_ROWS + 4 * LAYERS


def wait(eng, sem, value):
    if isinstance(value, int) and value <= 0:
        return
    eng.wait_ge(sem, value)


def groups(eng, step):
    for u in range(U):
        step(0, u)
    with eng.Fori(1, R - 1) as r:
        for u in range(U):
            step(r, u)
    for u in range(U):
        step(R - 1, u)


class At:

    def __init__(self, r, u, ahead=0):
        self.slot = (u + ahead) % U
        self.round = r + (u + ahead) // U
        self.g = r * U + u + ahead
        self.exists = not (isinstance(r, int) and not 0 <= self.g < G)
        self.last = isinstance(r, int) and self.g == G - 1
        self.two = self.slot % 2


class Chip:
    pass


class Tensors(ExitStack):

    def __init__(self, nc, k, phase):
        super().__init__()
        self.nc, self.phase, self.used = nc, phase + k.path, 0
        self.callback(self.clear)

    def sb(self, name, shape, dt=F32):
        return self.enter_context(self.nc.sbuf_tensor(f"{self.phase}_{name}", shape, dt))

    def ps(self, name, shape=(P, 512)):
        return self.enter_context(self.nc.psum_tensor(f"{self.phase}_{name}", list(shape), F32))

    def sem(self, name):
        sem = self.nc.alloc_semaphore(f"{self.phase}_{name}", num=FIRST_SEM + self.used)
        self.used += 1
        self.callback(self.nc.release_semaphore, sem)
        return sem

    def clear(self):
        if self.used:
            self.nc.all_engine_barrier(sems_to_clear=range(FIRST_SEM, FIRST_SEM + self.used))

    def sems(self, name, n):
        return [self.sem(f"{name}{i}") for i in range(n)]

    def block(self):
        return self.enter_context(self.nc.Block())


def mat(k, i, n=1):
    return k.mats[:, i * P:(i + n) * P]


def col(k, i):
    return k.cols[:, i:i + 1]


def chunk(t, c, n=CH):
    return t[:, c * CH:c * CH + n]



def prepare(nc, k):
    with Tensors(nc, k, "prep") as t:
        dsti = t.sb("dsti", [P, G * T], I32)
        dstf = t.sb("dstf", [P, G * T])
        first_i = t.sb("first_i", [1, G], I32)
        first = t.sb("first", [1, G])
        iota_i = t.sb("iota_i", [P, W], I32)
        part_i = t.sb("part_i", [P, 1], I32)
        part = t.sb("part", [P, 1])
        dist = t.sb("dist", [P, G * T])
        inside = t.sb("inside", [P, G * T])
        capped = t.sb("capped", [P, G * T])
        cosine = t.sb("cosine", [P, G * T])
        half_pi = t.sb("half_pi", [P, 1])
        far = t.sb("far", [P, G * T])
        before = t.sb("before", [P, G * T])
        real = t.sb("real", [P, G * T])
        misses = t.sb("misses", [P, 1])
        firsts = t.ps("firsts")
        total = t.ps("total")
        s_graph = t.sem("graph_loaded")
        s_load = t.sem("loaded")
        s_pool = t.sem("pool_made")
        s_ident = t.sem("ident_zeroed")
        s_dve = t.sem("dve_step")
        s_first = t.sem("first_ready")
        s_firsts = t.sem("firsts_spread")
        s_cos = t.sem("cosine_ready")
        s_dist = t.sem("dist_capped")
        s_miss = t.sem("misses_ready")
        s_total = t.sem("misses_summed")
        block = t.block()

        @block.sync
        def _(sp):
            sp.dma_start(dsti[:], k.dram["dst"]).then_inc(s_graph, 16)
            sp.dma_start(first_i[:], k.dram["dst_first"]).then_inc(s_graph, 16)
            sp.dma_start(dist[:], k.dram["dist"]).then_inc(s_graph, 16)
            sp.dma_start(k.mats[:], k.dram["mats"]).then_inc(s_load, 16)
            sp.dma_start(k.cols[:], k.dram["cols"]).then_inc(s_load, 16)
            sp.dma_start(k.rows[:], k.dram["rows"]).then_inc(s_load, 16)
            sp.dma_start(k.fw1[:], k.dram["fw1"]).then_inc(s_load, 16)
            sp.dma_start(k.x[:], k.dram["x"]).then_inc(s_load, 16)
            sp.dma_start(k.src[:], k.dram["src"]).then_inc(s_load, 16)
            sp.wait_ge(s_load, 96)

        @block.gpsimd
        def _(pool):
            pool.memset(k.ident[:], 0.0).then_inc(s_ident, 1)
            pool.wait_ge(s_ident, 1)
            pool.affine_select(out=k.ident[:], in_=k.ident[:], compare_op=ALU.not_equal, fill=1.0, base=0,
                               pattern=[[-1, P]], channel_multiplier=1).then_inc(s_pool, 1)
            pool.iota(iota_i[:], pattern=[[1, W]], base=0, channel_multiplier=0).then_inc(s_pool, 1)
            pool.iota(part_i[:], pattern=[[1, 1]], base=0, channel_multiplier=1).then_inc(s_pool, 1)

        @block.vector
        def _(dve):
            steps = [0]

            def then(instruction):
                steps[0] += 1
                instruction.then_inc(s_dve, 1)
                dve.wait_ge(s_dve, steps[0])

            dve.memset(k.ones[:], 1.0)
            dve.memset(k.mean_of[:], 1.0 / P)
            dve.memset(k.ln_eps[:], LN_EPS)
            then(dve.memset(half_pi[:], float(np.pi / 2)))
            dve.wait_ge(s_graph, 48)
            then(dve.tensor_scalar(first[:], first_i[:], float(NP - W), None, ALU.min))
            dve.tensor_copy(k.window[:], first[:]).then_inc(s_first, 1)
            then(dve.tensor_scalar(capped[:], dist[:], -1.0, None, ALU.mult))
            then(dve.tensor_tensor(capped[:], capped[:], dist[:], ALU.max))
            dve.tensor_scalar(capped[:], capped[:], CUTOFF, None, ALU.min).then_inc(s_dist, 1)
            then(dve.tensor_scalar(inside[:], dist[:], CUTOFF, None, ALU.is_le))
            dve.wait_ge(s_pool, 3)
            then(dve.tensor_copy(k.iota[:], iota_i[:]))
            then(dve.tensor_copy(part[:], part_i[:]))
            then(dve.tensor_scalar(k.minus_centre[:], part[:], -CUTOFF / (RBF - 1), None, ALU.mult))
            then(dve.tensor_copy(dstf[:], dsti[:]))
            dve.wait_ge(s_firsts, 1)
            for q in range(T):
                last = dve.tensor_tensor(k.place[:, q, :], dstf[:].rearrange("p (g q) -> p q g", q=T)[:, q, :],
                                         firsts[:, 0:G], ALU.subtract)
            then(last)
            placed = k.place[:].rearrange("p q g -> p (q g)")
            then(dve.tensor_copy(real[:].rearrange("p (q g) -> p q g", q=T), dstf[:].rearrange("p (g q) -> p q g", q=T)))
            then(dve.tensor_scalar(real[:], real[:], 0.0, None, ALU.is_ge))
            then(dve.tensor_scalar(far[:], placed, float(W), None, ALU.is_ge))
            then(dve.tensor_scalar(before[:], placed, 0.0, None, ALU.is_lt))
            then(dve.tensor_tensor(before[:], before[:], real[:], ALU.mult))
            then(dve.tensor_tensor(before[:], before[:], far[:], ALU.add))
            dve.tensor_reduce(misses[:], before[:], AX_X, ALU.max).then_inc(s_miss, 1)
            dve.wait_ge(s_cos, 1)
            then(dve.tensor_scalar(cosine[:], cosine[:], 1.0, 0.5, ALU.add, ALU.mult))
            dve.tensor_tensor(k.cut[:], cosine[:], inside[:], ALU.mult)
            dve.wait_ge(s_load, 96)
            dve.tensor_scalar(col(k, COLS["half_fb1"]), col(k, COLS["fb1"]), 0.5, None, ALU.mult)
            dve.tensor_scalar(col(k, COLS["half_mb1"]), col(k, COLS["mb1"]), 0.5, None, ALU.mult)
            dve.wait_ge(s_total, 1)
            dve.tensor_copy(k.missed[:], total[0:1, 0:1])

        @block.tensor
        def _(pe):
            pe.wait_ge(s_first, 1)
            pe.matmul(firsts[:, 0:G], k.ones[0:1, :], first[:], start=True, stop=True).then_inc(s_firsts, 1)
            pe.wait_ge(s_miss, 1)
            pe.matmul(total[0:1, 0:1], k.ones[:, 0:1], misses[:], start=True, stop=True).then_inc(s_total, 1)

        @block.scalar
        def _(act):
            act.wait_ge(s_dist, 1)
            act.wait_ge(s_dve, 1)
            act.activation(cosine[:], capped[:], ACT.Sin, bias=half_pi[:], scale=-float(np.pi) / CUTOFF).then_inc(s_cos, 1)



class Norm:

    def __init__(self, t, name, k, x, out, ps, ready, affine=False):
        self.k, self.x, self.out, self.ps, self.ready, self.affine = k, x, out, ps, ready, affine
        self.dev = t.dev
        self.sq = t.sq
        self.s_mean = t.sem(name + "_mean")
        self.s_dev = t.sem(name + "_deviation")
        self.s_sq = t.sem(name + "_square")
        self.s_var = t.sem(name + "_variance")
        self.s_std = t.sem(name + "_std")
        self.s_rstd = t.sem(name + "_rstd")
        self.s_scaled = t.sem(name + "_scaled")
        self.s_out = t.sem(name + "_normed")

    def tensor(self, pe):
        for c in range(NCH):
            pe.wait_ge(self.ready, c + 1)
            pe.matmul(self.ps[c][:, 0:CH], self.k.mean_of[:], chunk(self.x, c), start=True, stop=True).then_inc(self.s_mean, 1)
        for c in range(NCH):
            pe.wait_ge(self.s_sq, c + 1)
            pe.matmul(self.ps[c][:, 0:CH], self.k.mean_of[:], chunk(self.sq, c), start=True, stop=True).then_inc(self.s_var, 1)

    def scalar(self, act):
        for c in range(NCH):
            act.wait_ge(self.s_dev, c + 1)
            act.activation(chunk(self.sq, c), chunk(self.dev, c), ACT.Square).then_inc(self.s_sq, 1)
        for c in range(NCH):
            act.wait_ge(self.s_var, c + 1)
            act.activation(chunk(self.sq, c), self.ps[c][:, 0:CH], ACT.Sqrt, bias=self.k.ln_eps[:]).then_inc(self.s_std, 1)

    def vector(self, dve):
        for c in range(NCH):
            dve.wait_ge(self.s_mean, c + 1)
            dve.tensor_tensor(chunk(self.dev, c), chunk(self.x, c), self.ps[c][:, 0:CH], ALU.subtract).then_inc(self.s_dev, 1)
        for c in range(NCH):
            dve.wait_ge(self.s_std, c + 1)
            dve.reciprocal(chunk(self.sq, c), chunk(self.sq, c)).then_inc(self.s_rstd, 1)
            dve.wait_ge(self.s_rstd, c + 1)
            if self.affine:
                dve.tensor_tensor(chunk(self.dev, c), chunk(self.dev, c), chunk(self.sq, c), ALU.mult).then_inc(self.s_scaled, 1)
                dve.wait_ge(self.s_scaled, c + 1)
                dve.tensor_scalar(chunk(self.out, c), chunk(self.dev, c), col(self.k, COLS["gamma"]), col(self.k, COLS["beta"]),
                                  ALU.mult, ALU.add).then_inc(self.s_out, 1)
            else:
                dve.scalar_tensor_tensor(out=chunk(self.out, c), in0=chunk(self.dev, c), scalar=0.0, in1=chunk(self.sq, c),
                                         op0=ALU.max, op1=ALU.mult).then_inc(self.s_out, 1)


class Table:

    def __init__(self, t, k, h, ps, ready, weights, rows, outs, more=None):
        self.k, self.h, self.ps, self.ready, self.weights, self.rows, self.outs, self.more = k, h, ps, ready, weights, rows, outs, more
        self.width = weights.shape[1]
        self.stage = t.sb("table_stage", [P, NT, self.width])
        self.bias = t.sb("table_bias", [P, self.width]) if rows is not None else None
        self.s_bias_sum = t.sem("table_bias_sum")
        self.s_bias = t.sem("table_bias")
        self.s_rows = t.sem("table_rows")
        self.s_staged = t.sem("table_staged")
        self.s_stored = t.sem("table_stored")

    def tensor(self, pe):
        pe.wait_ge(self.ready, NCH)
        if self.rows is not None:
            pe.matmul(self.ps[7][:, 0:self.width], self.k.ones[0:1, :], self.rows, start=True, stop=self.more is None)
            if self.more is not None:
                pe.matmul(self.ps[7][:, 0:P], self.k.ones[0:1, :], self.more, start=False, stop=True)
            pe.matmul(self.ps[6][0:1, 0:1], self.k.ones[0:1, 0:1], self.k.ones[0:1, 0:1], start=True, stop=True).then_inc(self.s_bias_sum, 1)
        for j in range(NT):
            n = min(P, NP - j * P)
            wait(pe, self.s_staged, j - 3)
            pe.matmul(self.ps[j % 4][0:n, 0:self.width], self.h[:, j * P:j * P + n], self.weights,
                      start=True, stop=True).then_inc(self.s_rows, 1)

    def vector(self, dve):
        if self.rows is not None:
            dve.wait_ge(self.s_bias_sum, 1)
            dve.tensor_copy(self.bias[:], self.ps[7][:, 0:self.width]).then_inc(self.s_bias, 1)
            dve.wait_ge(self.s_bias, 1)
        for j in range(NT):
            n = min(P, NP - j * P)
            dve.wait_ge(self.s_rows, j + 1)
            if self.rows is not None:
                dve.tensor_tensor(self.stage[0:n, j, :], self.ps[j % 4][0:n, 0:self.width], self.bias[0:n, :], ALU.add).then_inc(self.s_staged, 1)
            else:
                dve.tensor_copy(self.stage[0:n, j, :], self.ps[j % 4][0:n, 0:self.width]).then_inc(self.s_staged, 1)

    def sync(self, sp):
        sp.wait_ge(self.s_staged, NT)
        whole = NP // P
        for dram, a, b in self.outs:
            sp.dma_start(dram[0:whole * P, :].rearrange("(j p) f -> p j f", p=P), self.stage[:, 0:whole, a:b]).then_inc(self.s_stored, 16)
            sp.dma_start(dram[whole * P:NP, :], self.stage[0:NP - whole * P, whole, a:b]).then_inc(self.s_stored, 16)
        sp.wait_ge(self.s_stored, 32 * len(self.outs))


def node_tensors(t):
    t.dev = t.sb("deviation", [P, NP])
    t.sq = t.sb("square", [P, NP])
    return [t.ps(f"bank{i}") for i in range(8)]


def nodes_first(nc, k):
    with Tensors(nc, k, "n0") as t:
        ps = node_tensors(t)
        s_x = t.sem("x_ready")
        norm = Norm(t, "norm", k, k.x, k.h, ps, s_x)
        table = Table(t, k, k.h, ps, norm.s_out, mat(k, MATS["pw"]), k.rows[:, ROWS["pb"] * P:(ROWS["pb"] + 1) * P], [(k.dram["t128"], 0, P)])
        s_row = t.sem("fb2_spread")
        block = t.block()

        @block.sync
        def _(sp):
            table.sync(sp)

        @block.gpsimd
        def _(pool):
            pool.sem_inc(s_x, NCH)

        @block.scalar
        def _(act):
            norm.scalar(act)

        @block.tensor
        def _(pe):
            pe.matmul(ps[7][:, 0:P], k.ones[0:1, :], k.rows[:, ROWS["fb2"] * P:(ROWS["fb2"] + 1) * P], start=True, stop=True).then_inc(s_row, 1)
            norm.tensor(pe)
            pe.wait_ge(s_row, 2)
            table.tensor(pe)

        @block.vector
        def _(dve):
            dve.wait_ge(s_row, 1)
            dve.tensor_copy(k.fb2[:], ps[7][:, 0:P]).then_inc(s_row, 1)
            norm.vector(dve)
            table.vector(dve)


def nodes_after_filter(nc, k):
    with Tensors(nc, k, "n1") as t:
        ps = node_tensors(t)
        half = t.sb("half", [P, NP])
        s_m1, s_half, s_tanh, s_silu, s_m2, s_x1, s_x = (t.sem(n) for n in ("m1", "half", "tanh", "silu", "m2", "x1", "x"))
        norm = Norm(t, "norm", k, k.x, k.h, ps, s_x)
        table = Table(t, k, k.h, ps, norm.s_out, k.ident[:], None, [(k.dram["t128"], 0, P)])
        block = t.block()

        @block.sync
        def _(sp):
            table.sync(sp)

        @block.scalar
        def _(act):
            for c in range(NCH):
                act.wait_ge(s_m1, c + 1)
                act.activation(chunk(half, c), ps[c][:, 0:CH], ACT.Identity, bias=col(k, COLS["half_mb1"]), scale=0.5).then_inc(s_half, 1)
                act.wait_ge(s_half, c + 1)
                act.activation(chunk(t.sq, c), chunk(half, c), ACT.Tanh).then_inc(s_tanh, 1)
            norm.scalar(act)

        @block.tensor
        def _(pe):
            for c in range(NCH):
                pe.matmul(ps[c][:, 0:CH], mat(k, MATS["mw1"]), k.acc[:, 0, c * CH:(c + 1) * CH], start=True, stop=True).then_inc(s_m1, 1)
            for c in range(NCH):
                pe.wait_ge(s_silu, c + 1)
                pe.matmul(ps[c][:, 0:CH], mat(k, MATS["mw2"]), chunk(half, c), start=True, stop=True).then_inc(s_m2, 1)
            norm.tensor(pe)
            table.tensor(pe)

        @block.vector
        def _(dve):
            for c in range(NCH):
                dve.wait_ge(s_tanh, c + 1)
                dve.scalar_tensor_tensor(out=chunk(half, c), in0=chunk(t.sq, c), scalar=1.0, in1=chunk(half, c),
                                         op0=ALU.add, op1=ALU.mult).then_inc(s_silu, 1)
            for c in range(NCH):
                dve.wait_ge(s_m2, c + 1)
                dve.scalar_tensor_tensor(out=chunk(k.x, c), in0=ps[c][:, 0:CH], scalar=col(k, COLS["mb2"]), in1=chunk(k.x, c),
                                         op0=ALU.add, op1=ALU.add).then_inc(s_x1, 1)
                dve.wait_ge(s_x1, c + 1)
                dve.tensor_tensor(chunk(k.x, c), chunk(k.x, c), chunk(k.h, c), ALU.add).then_inc(s_x, 1)
            norm.vector(dve)
            table.vector(dve)


def nodes_after_mean(nc, k):
    with Tensors(nc, k, "n2") as t:
        ps = node_tensors(t)
        s_deg, s_rdeg, s_mean, s_alone, s_m, s_relu, s_x = (t.sem(n) for n in ("deg", "rdeg", "mean", "alone", "m", "relu", "x"))
        s_hm = t.sem("hm")
        norm = Norm(t, "norm", k, k.x, k.h, ps, s_x)
        table = Table(t, k, k.h, ps, norm.s_out, k.ident[:], None, [(k.dram["t128"], 0, P)])
        block = t.block()

        @block.sync
        def _(sp):
            table.sync(sp)

        @block.scalar
        def _(act):
            for c in range(NCH):
                act.wait_ge(s_m, c + 1)
                act.activation(chunk(t.dev, c), ps[c][:, 0:CH], ACT.Relu, bias=col(k, COLS["L1"])).then_inc(s_relu, 1)
            norm.scalar(act)

        @block.tensor
        def _(pe):
            for c in range(NCH):
                pe.wait_ge(s_mean, c + 1)
                pe.matmul(ps[c][:, 0:CH], mat(k, MATS["L1"]), chunk(t.sq, c), start=True, stop=True).then_inc(s_m, 1)
            norm.tensor(pe)
            table.tensor(pe)

        @block.vector
        def _(dve):
            for c in range(NCH):
                total, deg = (k.acc[:, i, c * CH:(c + 1) * CH] for i in range(2))
                dve.tensor_scalar(chunk(t.sq, c), deg, 1.0, None, ALU.max).then_inc(s_deg, 1)
                dve.scalar_tensor_tensor(out=chunk(t.dev, c), in0=deg, scalar=0.0, in1=chunk(k.h, c),
                                         op0=ALU.is_equal, op1=ALU.mult).then_inc(s_alone, 1)
                dve.wait_ge(s_deg, c + 1)
                dve.reciprocal(chunk(t.sq, c), chunk(t.sq, c)).then_inc(s_rdeg, 1)
                dve.wait_ge(s_rdeg, c + 1)
                dve.tensor_tensor(chunk(t.sq, c), chunk(t.sq, c), total, ALU.mult).then_inc(s_hm, 1)
                dve.wait_ge(s_hm, c + 1)
                dve.wait_ge(s_alone, c + 1)
                dve.tensor_tensor(chunk(t.sq, c), chunk(t.sq, c), chunk(t.dev, c), ALU.add).then_inc(s_mean, 1)
            for c in range(NCH):
                dve.wait_ge(s_relu, c + 1)
                dve.tensor_tensor(chunk(k.x, c), chunk(k.x, c), chunk(t.dev, c), ALU.add).then_inc(s_x, 1)
            norm.vector(dve)
            table.vector(dve)


def layer_table(t, k, h, ps, ready, layer):
    a = (LAYER_ROWS + 4 * layer) * P
    return Table(t, k, h, ps, ready, mat(k, LAYER_MATS + 5 * layer, 3), k.rows[:, a:a + 3 * P],
                 [(k.dram["t256"], 0, 2 * P), (k.dram["t_dst"], 2 * P, 3 * P)], more=k.rows[:, a + 3 * P:a + 4 * P])


def nodes_after_sum(nc, k):
    with Tensors(nc, k, "n3") as t:
        ps = node_tensors(t)
        hid = t.sb("hid", [P, 2, CH])
        pre = k.acc[:, 1, :]
        s_hid, s_hidr, s_w2, s_pre1, s_pre, s_x, s_emb, s_h = (t.sem(n) for n in ("hid", "hidr", "w2", "pre1", "pre", "x", "emb", "h"))
        norm_out = Norm(t, "out", k, pre, t.dev, ps, s_pre, affine=True)
        norm = Norm(t, "norm", k, k.x, k.h, ps, s_x)
        table = layer_table(t, k, k.h, ps, s_h, 0)
        block = t.block()

        @block.sync
        def _(sp):
            table.sync(sp)

        @block.scalar
        def _(act):
            for n in range(4 * NCH):
                q = n % 4
                act.wait_ge(s_hid, n + 1)
                wait(act, s_w2, n - 1)
                act.activation(hid[:, n % 2, :], ps[n % 2][:, 0:CH], ACT.Relu, bias=col(k, COLS["b1"] + q)).then_inc(s_hidr, 1)
            norm_out.scalar(act)
            norm.scalar(act)
            for c in range(NCH):
                act.wait_ge(s_emb, c + 1)
                act.activation(chunk(k.h, c), ps[c][:, 0:CH], ACT.Identity, bias=col(k, COLS["emb_h"])).then_inc(s_h, 1)

        @block.tensor
        def _(pe):
            def up(n):
                c, q = n // 4, n % 4
                wait(pe, s_hidr, n - 1)
                pe.matmul(ps[n % 2][:, 0:CH], mat(k, MATS["W1"] + q), k.acc[:, 0, c * CH:(c + 1) * CH], start=True, stop=True).then_inc(s_hid, 1)

            up(0)
            for n in range(4 * NCH):
                c, q = n // 4, n % 4
                if n + 1 < 4 * NCH:
                    up(n + 1)
                pe.wait_ge(s_hidr, n + 1)
                if q == 0:
                    wait(pe, s_pre1, c - 1)
                pe.matmul(ps[2 + c % 2][:, 0:CH], mat(k, MATS["W2"] + q), hid[:, n % 2, :], start=q == 0, stop=q == 3).then_inc(s_w2, 1)
            norm_out.tensor(pe)
            norm.tensor(pe)
            for c in range(NCH):
                pe.wait_ge(norm.s_out, c + 1)
                pe.matmul(ps[c][:, 0:CH], mat(k, MATS["emb_h"]), chunk(k.h, c), start=True, stop=True).then_inc(s_emb, 1)
            table.tensor(pe)

        @block.vector
        def _(dve):
            for c in range(NCH):
                dve.wait_ge(s_w2, 4 * c + 4)
                dve.scalar_tensor_tensor(out=chunk(pre, c), in0=ps[2 + c % 2][:, 0:CH], scalar=col(k, COLS["b2"]), in1=chunk(k.h, c),
                                         op0=ALU.add, op1=ALU.add).then_inc(s_pre1, 1)
            dve.wait_ge(s_pre1, NCH)
            dve.sem_inc(s_pre, NCH)
            norm_out.vector(dve)
            for c in range(NCH):
                dve.wait_ge(norm_out.s_out, c + 1)
                dve.tensor_tensor(chunk(k.x, c), chunk(k.x, c), chunk(t.dev, c), ALU.add).then_inc(s_x, 1)
            norm.vector(dve)
            table.vector(dve)


def bn_terms(dve, act, t, k, which):
    raise NotImplementedError


def nodes_after_gates(nc, k, layer):
    final = layer == LAYERS - 1
    with Tensors(nc, k, f"n{4 + layer}") as t:
        ps = node_tensors(t)
        stats = t.sb("node_stats", [P, NCH, 6])
        moments = t.sb("moments", [P, 2, 2])
        std = t.sb("std", [P, 2])
        scale_node = t.sb("scale_node", [P, 1])
        shift_node = t.sb("shift_node", [P, 1])
        s_a, s_den, s_rden, s_gate, s_new, s_stats, s_relu, s_h, s_out = (
            t.sem(n) for n in ("a", "den", "rden", "gate", "new", "stats", "relu", "h", "out"))
        s_mom, s_std, s_dve = t.sem("moments"), t.sem("std"), t.sem("dve_step")
        s_bn = t.sem("bn_terms")
        if not final:
            table = layer_table(t, k, k.h, ps, s_h, layer + 1)
        c0 = LAYER_COLS + 5 * layer
        block = t.block()

        @block.sync
        def _(sp):
            if final:
                sp.wait_ge(s_h, NCH)
                sp.dma_start(k.dram["out"], k.x[:, 0:N]).then_inc(s_out, 16)
                sp.wait_ge(s_out, 16)
            else:
                table.sync(sp)

        @block.scalar
        def _(act):
            act.wait_ge(s_mom, 1)
            act.activation(std[:], moments[:, :, 1], ACT.Sqrt, bias=k.ln_eps[:]).then_inc(s_std, 1)
            act.wait_ge(s_bn, 1)
            for c in range(NCH):
                act.activation(chunk(t.sq, c), chunk(t.dev, c), ACT.Relu, bias=shift_node[:], scale=scale_node[:]).then_inc(s_relu, 1)

        @block.tensor
        def _(pe):
            for c in range(NCH):
                pe.matmul(ps[c][:, 0:CH], mat(k, LAYER_MATS + 5 * layer + 3), chunk(k.h, c), start=True, stop=True).then_inc(s_a, 1)
            if not final:
                table.tensor(pe)

        @block.vector
        def _(dve):
            steps = [0]

            def then(instruction):
                steps[0] += 1
                instruction.then_inc(s_dve, 1)
                dve.wait_ge(s_dve, steps[0])

            for c in range(NCH):
                num, den = (k.acc[:, i, c * CH:(c + 1) * CH] for i in range(2))
                dve.tensor_scalar(chunk(t.sq, c), den, 1e-6, None, ALU.add).then_inc(s_den, 1)
                dve.wait_ge(s_den, c + 1)
                dve.reciprocal(chunk(t.sq, c), chunk(t.sq, c)).then_inc(s_rden, 1)
                dve.wait_ge(s_rden, c + 1)
                dve.tensor_tensor(chunk(t.sq, c), chunk(t.sq, c), num, ALU.mult).then_inc(s_gate, 1)
                dve.wait_ge(s_gate, c + 1)
                dve.wait_ge(s_a, c + 1)
                dve.scalar_tensor_tensor(out=chunk(t.dev, c), in0=ps[c][:, 0:CH], scalar=col(k, c0), in1=chunk(t.sq, c),
                                         op0=ALU.add, op1=ALU.add).then_inc(s_new, 1)
                dve.wait_ge(s_new, c + 1)
                dve.bn_stats(stats[:, c, :], chunk(t.dev, c, LAST if c == NCH - 1 else CH)).then_inc(s_stats, 1)
            dve.wait_ge(s_stats, NCH)
            then(dve.bn_aggr(moments[:, 0, :], stats[:].rearrange("p c s -> p (c s)")))
            if final:
                then(dve.tensor_copy(moments[:, 1, :], moments[:, 0, :]))
            else:
                then(dve.bn_aggr(moments[:, 1, :], k.stats[:]))
            dve.sem_inc(s_mom, 1)
            dve.wait_ge(s_std, 1)
            then(dve.reciprocal(std[:], std[:]))
            then(dve.tensor_tensor(scale_node[:], std[:, 0:1], col(k, c0 + 1), ALU.mult))
            then(dve.tensor_tensor(shift_node[:], moments[:, 0, 0:1], scale_node[:], ALU.mult))
            then(dve.tensor_tensor(shift_node[:], col(k, c0 + 2), shift_node[:], ALU.subtract))
            if not final:
                then(dve.tensor_tensor(k.scale_edge[:], std[:, 1:2], col(k, c0 + 3), ALU.mult))
                then(dve.tensor_tensor(k.shift_edge[:], moments[:, 1, 0:1], k.scale_edge[:], ALU.mult))
                then(dve.tensor_tensor(k.shift_edge[:], col(k, c0 + 4), k.shift_edge[:], ALU.subtract))
            dve.sem_inc(s_bn, 1)
            for c in range(NCH):
                dve.wait_ge(s_relu, c + 1)
                if final:
                    then(dve.tensor_tensor(chunk(k.h, c), chunk(k.h, c), chunk(t.sq, c), ALU.add))
                    dve.tensor_tensor(chunk(k.x, c), chunk(k.x, c), chunk(k.h, c), ALU.add).then_inc(s_h, 1)
                else:
                    dve.tensor_tensor(chunk(k.h, c), chunk(k.h, c), chunk(t.sq, c), ALU.add).then_inc(s_h, 1)
            if not final:
                table.vector(dve)



def rows_count(k, j):
    each = 16 * T * k.gathers
    return k.gathered_before + each + each * j.round


def gather_rows(pool, k, t, table, rows, idx, s_idx, s_seen, s_rows, s_free, table_dst=None, rows_by_dst=None, idx_dst=None, s_idx_dst=None):
    by_dst = rows_by_dst is not None

    def step(r, u):
        j = At(r, u)
        wait(pool, s_free, j.g - U + 1)
        pool.wait_ge(s_idx, j.g + 1)
        pool.sem_inc(s_seen, 1)
        if by_dst:
            pool.tensor_copy(idx_dst[:, u * T:(u + 1) * T], k.dst_idx[:, bass.ds(j.g * T, T)]).then_inc(s_idx_dst, 1)
            pool.wait_ge(s_idx_dst, j.g + 1)
            pool.sem_inc(s_seen, 1)
        for q in range(T):
            pool.indirect_dma_start(out=rows[:, u, q, :], out_offset=None, in_=table,
                                    in_offset=bass.IndirectOffsetOnAxis(ap=idx[:, u * T + q:u * T + q + 1], axis=0)).then_inc(s_rows[u], 16)
            if by_dst:
                pool.indirect_dma_start(out=rows_by_dst[:, u, q, :], out_offset=None, in_=table_dst,
                                        in_offset=bass.IndirectOffsetOnAxis(ap=idx_dst[:, u * T + q:u * T + q + 1], axis=0)).then_inc(s_rows[u], 16)

    groups(pool, step)


def next_idx(dve, k, idx, s_idx, j):
    if j.exists:
        dve.tensor_copy(idx[:, j.slot * T:(j.slot + 1) * T], k.src[:, bass.ds(j.g * T, T)]).then_inc(s_idx, 1)


def first_idx(dve, k, idx, s_idx):
    for u in range(U):
        next_idx(dve, k, idx, s_idx, At(0, u))


def window_of(dve, k, g):
    if k.general:
        return None
    return dve.value_load(k.window[0:1, bass.ds(g, 1)], min_val=0, max_val=NP - W)


class Scatter:

    def __init__(self, t, k, blocks, scaled=False):
        self.k, self.blocks, self.scaled = k, blocks, scaled
        self.onehot = t.sb("onehot", [P, U, T, W])
        self.ps = [t.ps(f"sum{i}") for i in range(2)]
        self.s_zero = t.sem("zero")
        self.s_oh = t.sem("oh")
        self.s_sum = t.sem("sum")
        self.s_acc = t.sem("acc")
        self.s_enter = t.sem("enter")
        self.s_window = t.sem("window")

    def make(self, dve, out, j, iota):
        k = self.k
        if self.scaled:
            for q in range(T):
                last = dve.tensor_scalar(out[:, q, :], iota, k.place[:, q, bass.ds(j.g, 1)], k.cut[:, bass.ds(j.g * T + q, 1)],
                                         ALU.is_equal, ALU.mult)
        else:
            last = dve.tensor_tensor(out, k.place[:, :, bass.ds(j.g, 1)].broadcast_to([P, T, W]),
                                     iota.unsqueeze(1).broadcast_to([P, T, W]), ALU.is_equal)
        last.then_inc(self.s_oh, 1)

    def start(self, dve):
        dve.memset(self.k.acc[:], 0.0).then_inc(self.s_zero, 1)
        dve.wait_ge(self.s_zero, 1)
        if self.k.general:
            dve.sem_inc(self.s_acc, 1)

    def hot(self, dve, j):
        if j.exists and not self.k.general:
            wait(dve, self.s_sum, j.g - U + 1)
            self.make(dve, self.onehot[:, j.slot], j, self.k.iota[:])

    def products(self, pe, ps, slot, values):
        for a, tiles in enumerate(values):
            for n, (q, tile) in enumerate(tiles):
                last = pe.matmul(ps[:, a * W:(a + 1) * W], tile, self.onehot[:, slot, q, :], start=n == 0, stop=n == len(tiles) - 1)
        return last

    def tensor(self, pe, j, values):
        if not self.k.general:
            pe.wait_ge(self.s_oh, j.g + 1)
            wait(pe, self.s_acc, j.g - 1)
            self.products(pe, self.ps[j.two], j.slot, values).then_inc(self.s_sum, 1)
            return
        pe.sem_inc(self.s_enter, 1)
        with pe.Fori(0, NW) as w:
            pe.wait_ge(self.s_oh, j.g * NW + w + 1)
            pe.wait_ge(self.s_acc, j.g * NW + w + 1)
            self.products(pe, self.ps[0], 0, values).then_inc(self.s_window, 1)
        pe.wait_ge(self.s_window, (j.g + 1) * NW)
        pe.sem_inc(self.s_sum, 1)

    def add(self, dve, j):
        k, n = self.k, self.blocks
        if not j.exists:
            return
        if not k.general:
            window = window_of(dve, k, j.g)
            dve.wait_ge(self.s_sum, j.g + 1)
            wait(dve, self.s_acc, j.g)
            acc = k.acc[:, 0:n, bass.ds(window, W)]
            dve.tensor_tensor(acc, acc, self.ps[j.two][:, 0:n * W].rearrange("p (a w) -> p a w", a=n), ALU.add).then_inc(self.s_acc, 1)
            return
        dve.sem_inc(self.s_enter, 1)
        with dve.Fori(0, NW) as w:
            self.make(dve, self.onehot[:, 0], j, k.iota_all[:, bass.ds(w * W, W)])
            dve.wait_ge(self.s_window, j.g * NW + w + 1)
            dve.wait_ge(self.s_acc, j.g * NW + w + 1)
            acc = k.acc[:, 0:n, bass.ds(w * W, W)]
            dve.tensor_tensor(acc, acc, self.ps[0][:, 0:n * W].rearrange("p (a w) -> p a w", a=n), ALU.add).then_inc(self.s_acc, 1)


def edges_filter(nc, k):
    with Tensors(nc, k, "e0") as t:
        idx = t.sb("idx", [P, U * T], I32)
        rows = t.sb("rows", [P, U, T, P])
        dist = t.sb("dist", [RBF, U, GE])
        rbf = t.sb("rbf", [RBF, 2, GE])
        half = t.sb("half", [P, 2, GE])
        hid = t.sb("hid", [P, 2, GE])
        filt = t.sb("filt", [P, 2, T, P])
        ps_hid = [t.ps(f"hid{i}") for i in range(2)]
        ps_filt = [t.ps(f"filt{i}") for i in range(2)]
        scatter = Scatter(t, k, 1, scaled=True)
        s_idx, s_seen = t.sem("idx"), t.sem("seen")
        s_rows, s_dist = k.gathered, t.sems("dist", U)
        s_sq, s_rbf, s_up, s_half, s_tanh, s_hid, s_down, s_biased, s_msg = (
            t.sem(n) for n in ("sq", "rbf", "up", "half", "tanh", "hid", "down", "biased", "msg"))
        block = t.block()

        @block.gpsimd
        def _(pool):
            gather_rows(pool, k, t, k.dram["t128"], rows, idx, s_idx, s_seen, s_rows, s_msg)

        @block.sync
        def _(sp):
            def step(r, u):
                j = At(r, u)
                wait(sp, s_sq, j.g - U + 1)
                sp.dma_start(dist[:, u, :], k.dram["dist_row"][:, bass.ds(j.g * GE, GE)].broadcast_to([RBF, GE])).then_inc(s_dist[u], 16)

            groups(sp, step)

        @block.scalar
        def _(act):
            def basis(j):
                if not j.exists:
                    return
                act.wait_ge(s_dist[j.slot], 16 * (j.round + 1))
                wait(act, s_up, j.g - 1)
                act.activation(rbf[:, j.two, :], dist[:, j.slot, :], ACT.Square, bias=k.minus_centre[0:RBF, :]).then_inc(s_sq, 1)
                act.wait_ge(s_sq, j.g + 1)
                act.activation(rbf[:, j.two, :], rbf[:, j.two, :], ACT.Exp, scale=-1.0 / (2.0 * WIDTH * WIDTH)).then_inc(s_rbf, 1)

            def halves(j):
                if not j.exists:
                    return
                act.wait_ge(s_up, j.g + 1)
                wait(act, s_hid, j.g - 1)
                act.activation(half[:, j.two, :], ps_hid[j.two][:], ACT.Identity, bias=col(k, COLS["half_fb1"]), scale=0.5).then_inc(s_half, 1)
                act.wait_ge(s_half, j.g + 1)
                wait(act, s_down, j.g - 1)
                act.activation(hid[:, j.two, :], half[:, j.two, :], ACT.Tanh).then_inc(s_tanh, 1)

            basis(At(0, 0))
            basis(At(0, 1))
            halves(At(0, 0))
            basis(At(0, 2))
            halves(At(0, 1))

            def step(r, u):
                basis(At(r, u, 3))
                halves(At(r, u, 2))

            groups(act, step)

        @block.tensor
        def _(pe):
            def up(j):
                if not j.exists:
                    return
                pe.wait_ge(s_rbf, j.g + 1)
                wait(pe, s_half, j.g - 1)
                pe.matmul(ps_hid[j.two][:], k.fw1[:], rbf[:, j.two, :], start=True, stop=True).then_inc(s_up, 1)

            def down(j):
                if not j.exists:
                    return
                pe.wait_ge(s_hid, j.g + 1)
                wait(pe, s_biased, j.g - 1)
                for q in range(T):
                    last = pe.matmul(ps_filt[j.two][:, q * P:(q + 1) * P], hid[:, j.two, q * P:(q + 1) * P], mat(k, MATS["fw2"]), start=True, stop=True)
                last.then_inc(s_down, 1)

            def sums(j):
                if not j.exists:
                    return
                pe.wait_ge(s_msg, j.g + 1)
                scatter.tensor(pe, j, [[(q, filt[:, j.two, q, :]) for q in range(T)]])

            up(At(0, 0))
            up(At(0, 1))
            down(At(0, 0))
            up(At(0, 2))
            down(At(0, 1))

            def step(r, u):
                sums(At(r, u, -1))
                up(At(r, u, 3))
                down(At(r, u, 2))

            groups(pe, step)
            sums(At(R - 1, U - 1))

        @block.vector
        def _(dve):
            def hidden(j):
                if not j.exists:
                    return
                dve.wait_ge(s_tanh, j.g + 1)
                dve.scalar_tensor_tensor(out=hid[:, j.two, :], in0=hid[:, j.two, :], scalar=1.0, in1=half[:, j.two, :],
                                         op0=ALU.add, op1=ALU.mult).then_inc(s_hid, 1)

            def step(r, u):
                j = At(r, u)
                hidden(At(r, u, 2))
                scatter.hot(dve, At(r, u, 1))
                dve.wait_ge(s_down, j.g + 1)
                wait(dve, scatter.s_sum, j.g - 1)
                dve.tensor_tensor(filt[:, j.two], ps_filt[j.two][:].rearrange("p (q f) -> p q f", q=T),
                                  k.fb2[:].unsqueeze(1).broadcast_to([P, T, P]), ALU.add).then_inc(s_biased, 1)
                dve.wait_ge(s_biased, j.g + 1)
                dve.wait_ge(s_rows[u], rows_count(k, j))
                dve.tensor_tensor(filt[:, j.two], filt[:, j.two], rows[:, u], ALU.mult).then_inc(s_msg, 1)
                next_idx(dve, k, idx, s_idx, At(r, u, U))
                scatter.add(dve, At(r, u, -2))

            first_idx(dve, k, idx, s_idx)
            scatter.start(dve)
            scatter.hot(dve, At(0, 0))
            hidden(At(0, 0))
            hidden(At(0, 1))
            groups(dve, step)
            scatter.add(dve, At(R - 1, U - 2))
            scatter.add(dve, At(R - 1, U - 1))


def edges_sum(nc, k, with_edges):
    with Tensors(nc, k, "e2" if with_edges else "e1") as t:
        idx = t.sb("idx", [P, U * T], I32)
        rows = t.sb("rows", [P, U, T, P])
        edge = t.sb("edge", [P, U, T, P]) if with_edges else None
        scatter = Scatter(t, k, 1 if with_edges else 2)
        s_idx, s_seen = t.sem("idx"), t.sem("seen")
        s_rows, s_edge = k.gathered, t.sems("edge", U)
        block = t.block()

        @block.gpsimd
        def _(pool):
            gather_rows(pool, k, t, k.dram["t128"], rows, idx, s_idx, s_seen, s_rows, scatter.s_sum)

        if with_edges:
            @block.sync
            def _(sp):
                def step(r, u):
                    j = At(r, u)
                    wait(sp, scatter.s_sum, j.g - U + 1)
                    sp.dma_start(edge[:, u], k.dram["attr"][bass.ds(j.g * GE, GE), :].rearrange("(q p) f -> p q f", p=P)).then_inc(s_edge[u], 16)

                groups(sp, step)

        @block.tensor
        def _(pe):
            def step(r, u):
                j = At(r, u)
                pe.wait_ge(s_rows[u], rows_count(k, j))
                by_src = [(q, rows[:, u, q, :]) for q in range(T)]
                if with_edges:
                    pe.wait_ge(s_edge[u], 16 * (j.round + 1))
                    scatter.tensor(pe, j, [by_src + [(q, edge[:, u, q, :]) for q in range(T)]])
                else:
                    scatter.tensor(pe, j, [by_src, [(q, k.ones[:]) for q in range(T)]])

            groups(pe, step)

        @block.vector
        def _(dve):
            def step(r, u):
                scatter.hot(dve, At(r, u, 1))
                scatter.add(dve, At(r, u))
                next_idx(dve, k, idx, s_idx, At(r, u, U))

            first_idx(dve, k, idx, s_idx)
            scatter.start(dve)
            scatter.hot(dve, At(0, 0))
            groups(dve, step)


def edges_gates(nc, k, layer):
    final = layer == LAYERS - 1
    embeds = layer < 2
    keeps = layer in (1, 2)
    with Tensors(nc, k, f"g{layer}") as t:
        idx = t.sb("idx", [P, U * T], I32)
        rows = t.sb("rows", [P, U, T, 2 * P])
        dst_rows = t.sb("dst_rows", [W, U, P])
        e_in = t.sb("e_in", [P, U, GE])
        new_in = t.sb("new_in", [P, U, GE]) if layer else None
        relu = t.sb("relu", [P, 2, GE]) if layer else None
        e = t.sb("e", [P, U, GE])
        rows_by_dst = t.sb("rows_by_dst", [P, U, T, P]) if k.general else None
        idx_dst = t.sb("idx_dst", [P, U * T], I32) if k.general else None
        scatter = Scatter(t, k, 2)
        onehot_t = t.sb("onehot_t", [W, 2, GE])
        new = t.sb("new", [P, 2, T, P])
        sig = t.sb("sig", [P, 2, T, P])
        gated = t.sb("gated", [P, 2, T, P])
        new_t = t.sb("new_t", [P, U, GE])
        stat4 = t.sb("stat4", [P, U, 6])
        ps_new = [t.ps(f"new{i}") for i in range(2)]
        ps_t = [t.ps(f"t{i}") for i in range(2)]
        ps_oh = t.ps("oh")
        ps_emb = t.ps("emb")
        s_idx, s_seen, s_turning, s_by_src, s_idx_dst = t.sem("idx"), t.sem("seen"), t.sem("turning"), t.sem("by_src"), t.sem("idx_dst")
        s_rows, s_load = k.gathered, t.sems("load", U)
        s_keep_e, s_keep_new = t.sems("keep_e", U), t.sems("keep_new", U)
        s_turn, s_oht, s_emb, s_relu, s_e, s_ce, s_new, s_sig, s_gated, s_t, s_newt, s_bn, s_stat = (
            t.sem(n) for n in ("turn", "oht", "emb", "relu", "e", "ce", "new", "sig", "gated", "t", "newt", "bn", "stat"))
        loads = 1 + (layer > 0) + (not k.general)
        e_src = k.dram["attr_t"] if embeds else k.dram[f"e{layer - 1}"]
        wC = mat(k, LAYER_MATS + 5 * layer + 4)
        block = t.block()

        @block.gpsimd
        def _(pool):
            gather_rows(pool, k, t, k.dram["t256"], rows, idx, s_idx, s_seen, s_rows, s_gated, k.dram["t_dst"], rows_by_dst, idx_dst, s_idx_dst)

        @block.sync
        def _(sp):
            def load(j):
                if not j.exists:
                    return
                window = window_of(sp, k, j.g)
                wait(sp, s_ce, j.g - U + 1)
                sp.dma_start(e_in[:, j.slot, :], e_src[:, bass.ds(j.g * GE, GE)]).then_inc(s_load[j.slot], 16)
                if layer:
                    sp.dma_start(new_in[:, j.slot, :], k.dram[f"new{layer - 1}"][:, bass.ds(j.g * GE, GE)]).then_inc(s_load[j.slot], 16)
                if not k.general:
                    sp.dma_start(dst_rows[:, j.slot, :], k.dram["t_dst"][bass.ds(window, W), :]).then_inc(s_load[j.slot], 16)

            for u in range(U):
                load(At(0, u))

            def step(r, u):
                j = At(r, u)
                load(At(r, u, U))
                if keeps:
                    sp.wait_ge(s_e, j.g + 1)
                    sp.dma_start(k.dram[f"e{layer}"][:, bass.ds(j.g * GE, GE)], e[:, u, :]).then_inc(s_keep_e[u], 16)
                if not final:
                    sp.wait_ge(s_newt, j.g + 1)
                    sp.dma_start(k.dram[f"new{layer}"][:, bass.ds(j.g * GE, GE)], new_t[:, u, :]).then_inc(s_keep_new[u], 16)

            groups(sp, step)
            for u in range(U):
                if keeps:
                    sp.wait_ge(s_keep_e[u], 16 * R)
                if not final:
                    sp.wait_ge(s_keep_new[u], 16 * R)

        @block.scalar
        def _(act):
            def relu_of(j):
                if not j.exists:
                    return
                if layer:
                    act.wait_ge(s_load[j.slot], 16 * loads * (j.round + 1))
                    wait(act, s_e, j.g - 1)
                    act.activation(relu[:, j.two, :], new_in[:, j.slot, :], ACT.Relu, bias=k.shift_edge[:], scale=k.scale_edge[:]).then_inc(s_relu, 1)
                else:
                    act.wait_ge(s_emb, j.g + 1)
                    wait(act, s_ce, j.g - U + 1)
                    act.activation(e[:, j.slot, :], ps_emb[:], ACT.Identity, bias=col(k, COLS["emb_e"])).then_inc(s_e, 1)

            def turned(j):
                if not j.exists or k.general:
                    return
                act.wait_ge(s_turn, j.g + 1)
                wait(act, s_ce, j.g - 1)
                act.activation(onehot_t[:, j.two, :], ps_oh[0:W, :], ACT.Copy).then_inc(s_oht, 1)

            relu_of(At(0, 0))
            turned(At(0, 0))
            relu_of(At(0, 1))
            turned(At(0, 1))
            relu_of(At(0, 2))

            def step(r, u):
                j = At(r, u)
                act.wait_ge(s_new, j.g + 1)
                wait(act, scatter.s_sum, j.g - 1)
                act.activation(sig[:, j.two], new[:, j.two], ACT.Sigmoid).then_inc(s_sig, 1)
                relu_of(At(r, u, 3))
                if not final:
                    act.wait_ge(s_t, j.g + 1)
                    wait(act, s_keep_new[u], 16 * j.round)
                    wait(act, s_bn, j.g - U + 1)
                    act.activation(new_t[:, u, :], ps_t[j.two][:], ACT.Copy).then_inc(s_newt, 1)
                turned(At(r, u, 2))

            groups(act, step)

        @block.tensor
        def _(pe):
            def turn(j):
                if not j.exists or k.general:
                    return
                pe.wait_ge(scatter.s_oh, j.g + 1)
                wait(pe, s_oht, j.g)
                pe.sem_inc(s_turning, 1)
                for q in range(T):
                    last = pe.transpose(ps_oh[0:W, q * P:(q + 1) * P], scatter.onehot[:, j.slot, q, :], k.ident[:])
                last.then_inc(s_turn, 1)

            def embed(j):
                if not j.exists or not embeds:
                    return
                pe.wait_ge(s_load[j.slot], 16 * loads * (j.round + 1))
                wait(pe, s_e, j.g)
                pe.matmul(ps_emb[:], mat(k, MATS["emb_e"]), e_in[:, j.slot, :], start=True, stop=True).then_inc(s_emb, 1)

            def edge_terms(j):
                if not j.exists:
                    return
                if not k.general:
                    pe.wait_ge(s_oht, j.g + 1)
                pe.wait_ge(s_load[j.slot], 16 * loads * (j.round + 1))
                pe.wait_ge(s_e, j.g + 1)
                wait(pe, s_new, j.g - 1)
                for q in range(T):
                    cols = ps_new[j.two][:, q * P:(q + 1) * P]
                    if not k.general:
                        pe.matmul(cols, onehot_t[:, j.two, q * P:(q + 1) * P], dst_rows[:, j.slot, :], start=True, stop=False)
                    last = pe.matmul(cols, e[:, j.slot, q * P:(q + 1) * P], wC, start=k.general, stop=True)
                last.then_inc(s_ce, 1)

            def sums(j):
                if not j.exists:
                    return
                pe.wait_ge(s_gated, j.g + 1)
                scatter.tensor(pe, j, [[(q, values[:, j.two, q, :]) for q in range(T)] for values in (gated, sig)])

            embed(At(0, 0))
            turn(At(0, 0))
            embed(At(0, 1))
            turn(At(0, 1))
            edge_terms(At(0, 0))
            embed(At(0, 2))

            def step(r, u):
                j = At(r, u)
                edge_terms(At(r, u, 1))
                if not final:
                    pe.wait_ge(s_new, j.g + 1)
                    wait(pe, s_newt, j.g - 1)
                    for q in range(T):
                        last = pe.transpose(ps_t[j.two][:, q * P:(q + 1) * P], new[:, j.two, q, :], k.ident[:])
                    last.then_inc(s_t, 1)
                turn(At(r, u, 2))
                sums(At(r, u, -1))
                embed(At(r, u, 3))

            groups(pe, step)
            sums(At(R - 1, U - 1))

        @block.vector
        def _(dve):
            def edge(j):
                if not j.exists or not layer:
                    return
                dve.wait_ge(s_relu, j.g + 1)
                if keeps:
                    wait(dve, s_keep_e[j.slot], 16 * j.round)
                wait(dve, s_ce, j.g - U + 1)
                if embeds:
                    dve.wait_ge(s_emb, j.g + 1)
                    dve.scalar_tensor_tensor(out=e[:, j.slot, :], in0=ps_emb[:], scalar=col(k, COLS["emb_e"]), in1=relu[:, j.two, :],
                                             op0=ALU.add, op1=ALU.add).then_inc(s_e, 1)
                else:
                    dve.wait_ge(s_load[j.slot], 16 * loads * (j.round + 1))
                    dve.tensor_tensor(e[:, j.slot, :], e_in[:, j.slot, :], relu[:, j.two, :], ALU.add).then_inc(s_e, 1)

            first_idx(dve, k, idx, s_idx)
            scatter.start(dve)
            scatter.hot(dve, At(0, 0))
            scatter.hot(dve, At(0, 1))
            edge(At(0, 0))
            edge(At(0, 1))

            def counted(j):
                if final or not j.exists:
                    return
                dve.wait_ge(s_newt, j.g + 1)
                wait(dve, s_stat, j.round)
                dve.bn_stats(stat4[:, j.slot, :], new_t[:, j.slot, 0:ELAST if j.last else GE]).then_inc(s_bn, 1)
                if j.slot == U - 1:
                    dve.wait_ge(s_bn, j.g + 1)
                    dve.tensor_scalar(k.stats[:, bass.ds(j.round * U * 6, U * 6)], stat4[:].rearrange("p u s -> p (u s)"), 1.0, None,
                                      ALU.mult).then_inc(s_stat, 1)

            def step(r, u):
                j = At(r, u)
                scatter.hot(dve, At(r, u, 2))
                dve.wait_ge(s_ce, j.g + 1)
                dve.wait_ge(s_rows[u], rows_count(k, j))
                edge_terms = ps_new[j.two][:].rearrange("p (q f) -> p q f", q=T)
                if k.general:
                    dve.tensor_tensor(new[:, j.two], edge_terms, rows[:, u, :, 0:P], ALU.add).then_inc(s_by_src, 1)
                    dve.wait_ge(s_by_src, j.g + 1)
                    dve.tensor_tensor(new[:, j.two], new[:, j.two], rows_by_dst[:, u], ALU.add).then_inc(s_new, 1)
                else:
                    dve.tensor_tensor(new[:, j.two], edge_terms, rows[:, u, :, 0:P], ALU.add).then_inc(s_new, 1)
                edge(At(r, u, 2))
                dve.wait_ge(s_sig, j.g + 1)
                wait(dve, scatter.s_sum, j.g - 1)
                dve.tensor_tensor(gated[:, j.two], sig[:, j.two], rows[:, u, :, P:2 * P], ALU.mult).then_inc(s_gated, 1)
                next_idx(dve, k, idx, s_idx, At(r, u, U))
                counted(At(r, u, -1))
                scatter.add(dve, At(r, u, -2))

            groups(dve, step)
            counted(At(R - 1, U - 1))
            scatter.add(dve, At(R - 1, U - 2))
            scatter.add(dve, At(R - 1, U - 1))


def all_windows(nc, k):
    with Tensors(nc, k, "all_windows") as t:
        iota_i = t.sb("iota_i", [P, NP], I32)
        dsti = t.sb("dsti", [P, G * T], I32)
        dstf = t.sb("dstf", [P, G * T])
        s_iota, s_dst, s_float, s_clamped = (t.sem(n) for n in ("iota", "dst", "float", "clamped"))
        block = t.block()

        @block.gpsimd
        def _(pool):
            pool.iota(iota_i[:], pattern=[[1, NP]], base=0, channel_multiplier=0).then_inc(s_iota, 1)

        @block.sync
        def _(sp):
            sp.dma_start(dsti[:], k.dram["dst"]).then_inc(s_dst, 16)

        @block.vector
        def _(dve):
            dve.wait_ge(s_iota, 1)
            dve.tensor_copy(k.iota_all[:], iota_i[:])
            dve.wait_ge(s_dst, 16)
            dve.tensor_copy(dstf[:], dsti[:]).then_inc(s_float, 1)
            dve.wait_ge(s_float, 1)
            dve.tensor_copy(k.place[:], dstf[:].rearrange("p (g q) -> p q g", q=T)).then_inc(s_float, 1)
            dve.wait_ge(s_float, 2)
            dve.tensor_scalar(dstf[:], dstf[:], 0.0, None, ALU.max).then_inc(s_clamped, 1)
            dve.wait_ge(s_clamped, 1)
            dve.tensor_copy(k.dst_idx[:], dstf[:])


def layers(nc, k, general):
    k.general, k.gathers, k.gathered_before = general, 1, 0
    k.path = "_any" if general else "_in"
    with Tensors(nc, k, "tables") as t:
        if general:
            k.iota_all = t.sb("iota_all", [P, NP])
            k.dst_idx = t.sb("dst_idx", [P, G * T], I32)
            all_windows(nc, k)
        nodes_first(nc, k)
        edges_filter(nc, k)
        gathered(k)
        nodes_after_filter(nc, k)
        edges_sum(nc, k, False)
        gathered(k)
        nodes_after_mean(nc, k)
        edges_sum(nc, k, True)
        gathered(k)
        nodes_after_sum(nc, k)
        k.gathers = 2 if general else 1
        for layer in range(LAYERS):
            edges_gates(nc, k, layer)
            gathered(k)
            nodes_after_gates(nc, k, layer)


def gathered(k):
    k.gathered_before += 16 * T * k.gathers * R


def program(nc, dram):
    k = Chip()
    k.dram = dram
    k.path = ""
    with Tensors(nc, k, "all") as t:
        k.gathered = [t.enter_context(nc.semaphore(f"gathered{u}")) for u in range(U)]
        k.mats = t.sb("mats", [P, NMATS * P])
        k.cols = t.sb("cols", [P, NCOLS])
        k.rows = t.sb("bias_rows", [1, NROWS * P])
        k.fw1 = t.sb("fw1", [RBF, P])
        k.x = t.sb("x", [P, NP])
        k.h = t.sb("h", [P, NP])
        k.acc = t.sb("acc", [P, 2, NP])
        k.src = t.sb("src", [P, G * T], I32)
        k.window = t.sb("window", [1, G], I32)
        k.missed = t.sb("missed", [1, 1], I32)
        k.place = t.sb("place", [P, T, G])
        k.cut = t.sb("cut", [P, G * T])
        k.iota = t.sb("iota", [P, W])
        k.ident = t.sb("ident", [P, P])
        k.ones = t.sb("ones", [P, P])
        k.mean_of = t.sb("mean_of", [P, P])
        k.ln_eps = t.sb("ln_eps", [P, 1])
        k.minus_centre = t.sb("minus_centre", [P, 1])
        k.fb2 = t.sb("fb2", [P, P])
        k.stats = t.sb("stats", [P, G * 6])
        k.scale_edge = t.sb("scale_edge", [P, 1])
        k.shift_edge = t.sb("shift_edge", [P, 1])
        prepare(nc, k)
        missed = nc.values_load(k.missed[0:1, 0:1], min_val=0, max_val=P)
        with nc.If(missed == 0):
            layers(nc, k, False)
        with nc.Else():
            layers(nc, k, True)


def kernel(**inputs):
    import concourse.bacc as _bacc
    from concourse import mybir as _mybir
    from concourse.bass_utils import run_bass_kernel_spmd as _run

    a = {n: np.asarray(v) for n, v in inputs.items()}

    def tiles(v, fill):
        padded = np.full(EP, fill, v.dtype)
        padded[:E] = v
        return padded

    def column(v):
        return v.reshape(-1, P).T

    attr = np.zeros((EP, P), a["edge_attr_128"].dtype)
    attr[:E] = a["edge_attr_128"]
    x = np.zeros((P, NP), a["x"].dtype)
    x[:, :N] = a["x"].T
    src, dst, dist = tiles(a["src"], 0), tiles(a["dst"], -1), tiles(a["edge_weight"], 0)
    mats = [a["L0_gnn_fw2"], a["L0_gnn_pw"], a["L0_gnn_mw1"], a["L0_gnn_mw2"], a["L1_gnn_W"], a["L2_gnn_W1"]]
    mats += [a["L2_gnn_W2"][q * P:(q + 1) * P] for q in range(4)] + [a["L3_gnn_W_emb_h"], a["L3_gnn_W_emb_e"]]
    mats += [a[f"L3_gnn_{m}w"][layer] for layer in range(LAYERS) for m in "DBEAC"]
    cols = [a["L0_gnn_fb1"], a["L0_gnn_mb1"], a["L0_gnn_mb2"], a["L1_gnn_b"], a["L2_gnn_b1"], a["L2_gnn_b2"], a["L2_gnn_gamma"],
            a["L2_gnn_beta"], a["L3_gnn_b_emb_h"], a["L3_gnn_b_emb_e"], np.zeros(2 * P, np.float32)]
    cols += [a[f"L3_gnn_{m}"][layer] for layer in range(LAYERS) for m in ("Ab", "gh", "bh", "ge", "be")]
    rows = [a["L0_gnn_pb"], a["L0_gnn_fb2"]] + [a[f"L3_gnn_{m}b"][layer] for layer in range(LAYERS) for m in "DBEC"]
    arrays = {
        "x": x,
        "src": src.reshape(-1, P).T,
        "dst": dst.reshape(-1, P).T,
        "dst_first": dst.reshape(1, G, GE)[:, :, 0],
        "dist": dist.reshape(-1, P).T,
        "dist_row": dist.reshape(1, EP),
        "attr": attr,
        "attr_t": attr.T,
        "fw1": a["L0_gnn_fw1"],
        "mats": np.concatenate(mats, axis=1),
        "cols": np.concatenate([column(c) for c in cols], axis=1),
        "rows": np.concatenate(rows).reshape(1, -1),
    }
    arrays = {f"in_{n}": np.ascontiguousarray(v) for n, v in arrays.items()}
    nc = _bacc.Bacc("TRN2", target_bir_lowering=False, num_devices=1)
    dram = {n[3:]: nc.dram_tensor(n, v.shape, _mybir.dt.from_np(v.dtype), kind="ExternalInput").ap() for n, v in arrays.items()}
    scratch = {"t128": (NP, P), "t256": (NP, 2 * P), "t_dst": (NP, P), "e1": (P, EP), "e2": (P, EP), "new0": (P, EP), "new1": (P, EP), "new2": (P, EP)}
    for n, shape in scratch.items():
        dram[n] = nc.dram_tensor(n, shape, _mybir.dt.float32).ap()
    dram["out"] = nc.dram_tensor("out_x", (P, N), _mybir.dt.float32, kind="ExternalOutput").ap()
    program(nc, dram)
    result = _run(nc, [arrays], core_ids=[0])
    return np.ascontiguousarray(result.results[0]["out_x"].T)
```

```python
from contextlib import ExitStack

import numpy as np
import concourse.bass as bass
from concourse import mybir
from concourse.alu_op_type import AluOpType as ALU

F32 = mybir.dt.float32
I32 = mybir.dt.int32
ACT = mybir.ActivationFunctionType
AX_X = mybir.AxisListType.X

P = 128
N = 3125
W = 64
NW = -(-N // W)
NP = NW * W
CH = 512
NCH = -(-NP // CH)
LAST = N - (NCH - 1) * CH
NT = -(-NP // P)
WARM = 7
STORED = 4
E = 53125
T = 4
GE = T * P
G = -(-E // GE)
EP = G * GE
ELAST = E - (G - 1) * GE
U = 4
R = G // U
FIRST_SEM = 128
RBF = 50
CUTOFF = 10.0
WIDTH = CUTOFF / RBF * 0.5
LAYERS = 4
LN_EPS = 1e-5
BN_EPS = 1e-5
GATE_EPS = 1e-6
TC = CH // P
assert G % U == 0 and NCH <= 7 and LN_EPS == BN_EPS

MATS = {"fw2": 0, "pw": 1, "mw1": 2, "mw2": 3, "L1": 4, "W1": 5, "W2": 9, "emb_h": 13, "emb_e": 14}
LAYER_MATS = 15
NMATS = LAYER_MATS + 5 * LAYERS
COLS = {"fb1": 0, "mb1": 1, "mb2": 2, "L1": 3, "b1": 4, "b2": 8, "gamma": 9, "beta": 10, "emb_h": 11,
        "emb_e": 12, "half_fb1": 13, "half_mb1": 14}
LAYER_COLS = 15
NCOLS = LAYER_COLS + 5 * LAYERS
ROWS = {"pb": 0, "fb2": 1}
LAYER_ROWS = 2
NROWS = LAYER_ROWS + 4 * LAYERS


def wait(eng, sem, value):
    if isinstance(value, int) and value <= 0:
        return
    eng.wait_ge(sem, value)


def groups(eng, step):
    for u in range(U):
        step(0, u)
    with eng.Fori(1, R - 1) as r:
        for u in range(U):
            step(r, u)
    for u in range(U):
        step(R - 1, u)


class At:

    def __init__(self, r, u, ahead=0):
        self.slot = (u + ahead) % U
        self.round = r + (u + ahead) // U
        self.g = r * U + u + ahead
        self.exists = not (isinstance(r, int) and not 0 <= self.g < G)
        self.last = isinstance(r, int) and self.g == G - 1
        self.two = self.slot % 2


class Chip:
    pass


class Tensors(ExitStack):

    def __init__(self, nc, k, phase):
        super().__init__()
        self.nc, self.phase, self.used = nc, phase + k.path, 0
        self.callback(self.clear)

    def sb(self, name, shape, dt=F32):
        return self.enter_context(self.nc.sbuf_tensor(f"{self.phase}_{name}", shape, dt))

    def ps(self, name, shape=(P, 512)):
        return self.enter_context(self.nc.psum_tensor(f"{self.phase}_{name}", list(shape), F32))

    def sem(self, name):
        sem = self.nc.alloc_semaphore(f"{self.phase}_{name}", num=FIRST_SEM + self.used)
        self.used += 1
        self.callback(self.nc.release_semaphore, sem)
        return sem

    def clear(self):
        if self.used:
            self.nc.all_engine_barrier(sems_to_clear=range(FIRST_SEM, FIRST_SEM + self.used))

    def sems(self, name, n):
        return [self.sem(f"{name}{i}") for i in range(n)]

    def block(self):
        return self.enter_context(self.nc.Block())


def mat(k, i, n=1):
    return k.mats[:, i * P:(i + n) * P]


def col(k, i):
    return k.cols[:, i:i + 1]


def size(c):
    return min(CH, NP - c * CH)


def chunk(t, c, n=None):
    return t[:, c * CH:c * CH + (size(c) if n is None else n)]



def prepare(nc, k):
    with Tensors(nc, k, "prep") as t:
        dsti = t.sb("dsti", [P, G * T], I32)
        dstf = t.sb("dstf", [P, G * T])
        first_i = t.sb("first_i", [1, G], I32)
        first = t.sb("first", [1, G])
        iota_i = t.sb("iota_i", [P, W], I32)
        part_i = t.sb("part_i", [P, 1], I32)
        part = t.sb("part", [P, 1])
        dist = t.sb("dist", [P, G * T])
        inside = t.sb("inside", [P, G * T])
        capped = t.sb("capped", [P, G * T])
        cosine = t.sb("cosine", [P, G * T])
        half_pi = t.sb("half_pi", [P, 1])
        far = t.sb("far", [P, G * T])
        before = t.sb("before", [P, G * T])
        real = t.sb("real", [P, G * T])
        misses = t.sb("misses", [P, 1])
        firsts = t.ps("firsts")
        total = t.ps("total")
        s_graph = t.sem("graph_loaded")
        s_load = t.sem("loaded")
        s_pool = t.sem("pool_made")
        s_ident = t.sem("ident_zeroed")
        s_dve = t.sem("dve_step")
        s_first = t.sem("first_ready")
        s_firsts = t.sem("firsts_spread")
        s_cos = t.sem("cosine_ready")
        s_dist = t.sem("dist_capped")
        s_miss = t.sem("misses_ready")
        s_total = t.sem("misses_summed")
        block = t.block()

        @block.sync
        def _(sp):
            sp.dma_start(dsti[:], k.dram["dst"]).then_inc(s_graph, 16)
            sp.dma_start(first_i[:], k.dram["dst_first"]).then_inc(s_graph, 16)
            sp.dma_start(dist[:], k.dram["dist"]).then_inc(s_graph, 16)
            sp.dma_start(k.mats[:], k.dram["mats"]).then_inc(s_load, 16)
            sp.dma_start(k.cols[:], k.dram["cols"]).then_inc(s_load, 16)
            sp.dma_start(k.rows[:], k.dram["rows"]).then_inc(s_load, 16)
            sp.dma_start(k.fw1[:], k.dram["fw1"]).then_inc(s_load, 16)
            sp.dma_start(k.x[:], k.dram["x"]).then_inc(s_load, 16)
            sp.dma_start(k.src[:], k.dram["src"]).then_inc(s_load, 16)
            sp.wait_ge(s_load, 96)

        @block.gpsimd
        def _(pool):
            pool.memset(k.ident[:], 0.0).then_inc(s_ident, 1)
            pool.wait_ge(s_ident, 1)
            pool.affine_select(out=k.ident[:], in_=k.ident[:], compare_op=ALU.not_equal, fill=1.0, base=0,
                               pattern=[[-1, P]], channel_multiplier=1).then_inc(s_pool, 1)
            pool.iota(iota_i[:], pattern=[[1, W]], base=0, channel_multiplier=0).then_inc(s_pool, 1)
            pool.iota(part_i[:], pattern=[[1, 1]], base=0, channel_multiplier=1).then_inc(s_pool, 1)

        @block.vector
        def _(dve):
            steps = [0]

            def then(instruction):
                steps[0] += 1
                instruction.then_inc(s_dve, 1)
                dve.wait_ge(s_dve, steps[0])

            dve.memset(k.ones[:], 1.0)
            dve.memset(k.mean_of[:], 1.0 / P)
            dve.memset(k.ln_eps[:], LN_EPS)
            dve.memset(k.gate_eps[:], GATE_EPS)
            then(dve.memset(half_pi[:], float(np.pi / 2)))
            dve.wait_ge(s_graph, 48)
            then(dve.tensor_scalar(first[:], first_i[:], float(NP - W), None, ALU.min))
            dve.tensor_copy(k.window[:], first[:]).then_inc(s_first, 1)
            then(dve.tensor_scalar(capped[:], dist[:], -1.0, None, ALU.mult))
            then(dve.tensor_tensor(capped[:], capped[:], dist[:], ALU.max))
            dve.tensor_scalar(capped[:], capped[:], CUTOFF, None, ALU.min).then_inc(s_dist, 1)
            then(dve.tensor_scalar(inside[:], dist[:], CUTOFF, None, ALU.is_le))
            dve.wait_ge(s_pool, 3)
            then(dve.tensor_copy(k.iota[:], iota_i[:]))
            then(dve.tensor_copy(part[:], part_i[:]))
            then(dve.tensor_scalar(k.minus_centre[:], part[:], -CUTOFF / (RBF - 1), None, ALU.mult))
            then(dve.tensor_copy(dstf[:], dsti[:]))
            dve.wait_ge(s_firsts, 1)
            for q in range(T):
                last = dve.tensor_tensor(k.place[:, q, :], dstf[:].rearrange("p (g q) -> p q g", q=T)[:, q, :],
                                         firsts[:, 0:G], ALU.subtract)
            then(last)
            placed = k.place[:].rearrange("p q g -> p (q g)")
            then(dve.tensor_copy(real[:].rearrange("p (q g) -> p q g", q=T), dstf[:].rearrange("p (g q) -> p q g", q=T)))
            then(dve.tensor_scalar(real[:], real[:], 0.0, None, ALU.is_ge))
            then(dve.tensor_scalar(far[:], placed, float(W), None, ALU.is_ge))
            then(dve.tensor_scalar(before[:], placed, 0.0, None, ALU.is_lt))
            then(dve.tensor_tensor(before[:], before[:], real[:], ALU.mult))
            then(dve.tensor_tensor(before[:], before[:], far[:], ALU.add))
            dve.tensor_reduce(misses[:], before[:], AX_X, ALU.max).then_inc(s_miss, 1)
            dve.wait_ge(s_cos, 1)
            then(dve.tensor_scalar(cosine[:], cosine[:], 1.0, 0.5, ALU.add, ALU.mult))
            dve.tensor_tensor(k.cut[:], cosine[:], inside[:], ALU.mult)
            dve.wait_ge(s_load, 96)
            dve.tensor_scalar(col(k, COLS["half_fb1"]), col(k, COLS["fb1"]), 0.5, None, ALU.mult)
            dve.tensor_scalar(col(k, COLS["half_mb1"]), col(k, COLS["mb1"]), 0.5, None, ALU.mult)
            dve.wait_ge(s_total, 1)
            dve.tensor_copy(k.missed[:], total[0:1, 0:1])

        @block.tensor
        def _(pe):
            pe.wait_ge(s_first, 1)
            pe.matmul(firsts[:, 0:G], k.ones[0:1, :], first[:], start=True, stop=True).then_inc(s_firsts, 1)
            pe.wait_ge(s_miss, 1)
            pe.matmul(total[0:1, 0:1], k.ones[:, 0:1], misses[:], start=True, stop=True).then_inc(s_total, 1)

        @block.scalar
        def _(act):
            act.wait_ge(s_dist, 1)
            act.wait_ge(s_dve, 1)
            act.activation(cosine[:], capped[:], ACT.Sin, bias=half_pi[:], scale=-float(np.pi) / CUTOFF).then_inc(s_cos, 1)



def inverse(act, t, c, s_log, s_done):
    act.wait_ge(s_log, c + 1)
    act.activation(chunk(t, c), chunk(t, c), ACT.Exp, scale=-1.0).then_inc(s_done, 1)


class Norm:

    def __init__(self, t, name, k, x, out, ps, ready, affine=False):
        self.k, self.x, self.out, self.ps, self.ready, self.affine = k, x, out, ps, ready, affine
        self.dev = t.dev
        self.sq = t.sq
        self.std = t.sb(name + "_std_columns", [P, NT])
        self.diag = t.diag
        self.s_mean = t.sem(name + "_mean")
        self.s_dev = t.sem(name + "_deviation")
        self.s_sq = t.sem(name + "_square")
        self.s_var = t.sem(name + "_variance")
        self.s_std = t.sem(name + "_std")
        self.s_rstd = t.sem(name + "_rstd")
        self.s_diag = t.sem(name + "_diag")
        self.s_spread = t.sem(name + "_spread")
        self.s_scaled = t.sem(name + "_scaled")
        self.s_out = t.sem(name + "_normed")

    def tiles(self, c):
        return range(c * TC, min((c + 1) * TC, NT))

    def rows(self, c):
        return min(P, size(c))

    def tensor(self, pe):
        for c in range(NCH):
            pe.wait_ge(self.ready, c + 1)
            pe.matmul(self.ps[c][:, 0:size(c)], self.k.mean_of[:], chunk(self.x, c), start=True, stop=True).then_inc(self.s_mean, 1)
        for c in range(NCH):
            pe.wait_ge(self.s_sq, c + 1)
            n = self.rows(c)
            for i, j in enumerate(self.tiles(c)):
                last = pe.matmul(self.ps[c][0:n, i:i + 1], self.sq[:, j * P:j * P + n], self.k.mean_of[:, 0:1],
                                 start=True, stop=True)
            last.then_inc(self.s_var, 1)
        for c in range(NCH):
            pe.wait_ge(self.s_diag, c + 1)
            n = self.rows(c)
            pe.matmul(self.ps[c][:, 0:size(c)], self.k.ones[0:n, :], self.diag[0:n, c, 0:size(c)], start=True, stop=True).then_inc(self.s_spread, 1)

    def scalar(self, act):
        for c in range(NCH):
            act.wait_ge(self.s_dev, c + 1)
            act.activation(chunk(self.sq, c), chunk(self.dev, c), ACT.Square).then_inc(self.s_sq, 1)
        for c in range(NCH):
            act.wait_ge(self.s_var, c + 1)
            n, at = self.rows(c), self.tiles(c)
            act.activation(self.std[0:n, at.start:at.stop], self.ps[c][0:n, 0:len(at)], ACT.Sqrt, bias=self.k.ln_eps[0:n, :]).then_inc(self.s_std, 1)
        if self.affine:
            for c in range(NCH):
                act.wait_ge(self.s_scaled, c + 1)
                act.activation(chunk(self.out, c), chunk(self.dev, c), ACT.Identity, bias=col(self.k, COLS["beta"]),
                               scale=col(self.k, COLS["gamma"])).then_inc(self.s_out, 1)

    def vector(self, dve):
        def diagonal(c):
            dve.wait_ge(self.s_std, c + 1)
            n, at = self.rows(c), self.tiles(c)
            std = self.std[0:n, at.start:at.stop]
            dve.reciprocal(std, std).then_inc(self.s_rstd, 1)
            dve.wait_ge(self.s_rstd, c + 1)
            dve.tensor_tensor(self.diag[0:n, c, 0:size(c)].rearrange("p (j n) -> p j n", n=n),
                              self.k.ident[0:n, 0:n].unsqueeze(1).broadcast_to([n, len(at), n]),
                              std.unsqueeze(2).broadcast_to([n, len(at), n]), ALU.mult).then_inc(self.s_diag, 1)

        for c in range(NCH):
            dve.wait_ge(self.s_mean, c + 1)
            dve.tensor_tensor(chunk(self.dev, c), chunk(self.x, c), self.ps[c][:, 0:size(c)], ALU.subtract).then_inc(self.s_dev, 1)
        diagonal(0)
        for c in range(NCH):
            if c + 1 < NCH:
                diagonal(c + 1)
            dve.wait_ge(self.s_spread, c + 1)
            if self.affine:
                dve.tensor_tensor(chunk(self.dev, c), chunk(self.dev, c), self.ps[c][:, 0:size(c)], ALU.mult).then_inc(self.s_scaled, 1)
            else:
                dve.scalar_tensor_tensor(out=chunk(self.out, c), in0=chunk(self.dev, c), scalar=0.0, in1=self.ps[c][:, 0:size(c)],
                                         op0=ALU.max, op1=ALU.mult).then_inc(self.s_out, 1)


class Table:

    def __init__(self, t, k, h, ps, ready, weights, rows, outs, more=None):
        self.k, self.h, self.ps, self.ready, self.weights, self.rows, self.outs, self.more = k, h, ps, ready, weights, rows, outs, more
        self.width = weights.shape[1]
        self.stage = t.sb("table_stage", [P, NT, self.width])
        self.bias = t.sb("table_bias", [P, self.width]) if rows is not None else None
        self.s_bias_sum = t.sem("table_bias_sum")
        self.s_bias = t.sem("table_bias")
        self.s_rows = t.sem("table_rows")
        self.s_staged = t.sem("table_staged")
        self.s_stored = t.sem("table_stored")

    def biases(self, pe):
        pe.matmul(self.ps[7][:, 0:self.width], self.k.ones[0:1, :], self.rows, start=True, stop=self.more is None)
        if self.more is not None:
            pe.matmul(self.ps[7][:, 0:P], self.k.ones[0:1, :], self.more, start=False, stop=True)
        pe.matmul(self.ps[7][0:1, 511:512], self.k.ones[0:1, 0:1], self.k.ones[0:1, 0:1], start=True, stop=True).then_inc(self.s_bias_sum, 1)

    def tensor(self, pe):
        for j in range(NT):
            n = min(P, NP - j * P)
            pe.wait_ge(self.ready, max((j * P + n - 1) // CH, j % 4) + 1)
            wait(pe, self.s_staged, j - 3)
            pe.matmul(self.ps[j % 4][0:n, 0:self.width], self.h[:, j * P:j * P + n], self.weights,
                      start=True, stop=True).then_inc(self.s_rows, 1)

    def spread(self, dve):
        dve.wait_ge(self.s_bias_sum, 1)
        dve.tensor_copy(self.bias[:], self.ps[7][:, 0:self.width]).then_inc(self.s_bias, 1)

    def vector(self, dve):
        if self.rows is not None:
            dve.wait_ge(self.s_bias, 1)
        for j in range(NT):
            n = min(P, NP - j * P)
            dve.wait_ge(self.s_rows, j + 1)
            if self.rows is not None:
                dve.tensor_tensor(self.stage[0:n, j, :], self.ps[j % 4][0:n, 0:self.width], self.bias[0:n, :], ALU.add).then_inc(self.s_staged, 1)
            else:
                dve.tensor_copy(self.stage[0:n, j, :], self.ps[j % 4][0:n, 0:self.width]).then_inc(self.s_staged, 1)

    def sync(self, sp):
        whole, stores = NP // P, 0
        for j in range(0, whole, STORED):
            n = min(STORED, whole - j)
            sp.wait_ge(self.s_staged, j + n)
            for dram, a, b in self.outs:
                sp.dma_start(dram[j * P:(j + n) * P, :].rearrange("(j p) f -> p j f", p=P), self.stage[:, j:j + n, a:b]).then_inc(self.s_stored, 16)
                stores += 1
        sp.wait_ge(self.s_staged, NT)
        for dram, a, b in self.outs:
            sp.dma_start(dram[whole * P:NP, :], self.stage[0:NP - whole * P, whole, a:b]).then_inc(self.s_stored, 16)
            stores += 1
        sp.wait_ge(self.s_stored, 16 * stores)


def node_tensors(t):
    t.dev = t.sb("deviation", [P, NP])
    t.sq = t.sb("square", [P, NP])
    t.diag = t.sb("diagonal", [P, NCH, CH])
    return [t.ps(f"bank{i}") for i in range(8)]


def nodes_first(nc, k):
    with Tensors(nc, k, "n0") as t:
        ps = node_tensors(t)
        s_x = t.sem("x_ready")
        norm = Norm(t, "norm", k, k.x, k.h, ps, s_x)
        table = Table(t, k, k.h, ps, norm.s_out, mat(k, MATS["pw"]), k.rows[:, ROWS["pb"] * P:(ROWS["pb"] + 1) * P], [(k.dram["t128"], 0, P)])
        s_row = t.sem("fb2_spread")
        block = t.block()

        @block.sync
        def _(sp):
            table.sync(sp)

        @block.gpsimd
        def _(pool):
            pool.sem_inc(s_x, NCH)

        @block.scalar
        def _(act):
            norm.scalar(act)

        @block.tensor
        def _(pe):
            pe.matmul(ps[7][:, 0:P], k.ones[0:1, :], k.rows[:, ROWS["fb2"] * P:(ROWS["fb2"] + 1) * P], start=True, stop=True).then_inc(s_row, 1)
            pe.wait_ge(s_row, 2)
            table.biases(pe)
            norm.tensor(pe)
            table.tensor(pe)

        @block.vector
        def _(dve):
            dve.wait_ge(s_row, 1)
            dve.tensor_copy(k.fb2[:], ps[7][:, 0:P]).then_inc(s_row, 1)
            table.spread(dve)
            norm.vector(dve)
            table.vector(dve)


def nodes_after_filter(nc, k):
    with Tensors(nc, k, "n1") as t:
        ps = node_tensors(t)
        half = t.sb("half", [P, NP])
        s_m1, s_half, s_tanh, s_silu, s_m2, s_x1, s_x = (t.sem(n) for n in ("m1", "half", "tanh", "silu", "m2", "x1", "x"))
        norm = Norm(t, "norm", k, k.x, k.h, ps, s_x)
        table = Table(t, k, k.h, ps, norm.s_out, k.ident[:], None, [(k.dram["t128"], 0, P)])
        block = t.block()

        @block.sync
        def _(sp):
            table.sync(sp)

        @block.scalar
        def _(act):
            for c in range(NCH):
                act.wait_ge(s_m1, c + 1)
                act.activation(chunk(half, c), ps[c][:, 0:size(c)], ACT.Identity, bias=col(k, COLS["half_mb1"]), scale=0.5).then_inc(s_half, 1)
                act.wait_ge(s_half, c + 1)
                act.activation(chunk(t.sq, c), chunk(half, c), ACT.Tanh).then_inc(s_tanh, 1)
            norm.scalar(act)

        @block.tensor
        def _(pe):
            for c in range(NCH):
                pe.matmul(ps[c][:, 0:size(c)], mat(k, MATS["mw1"]), chunk(k.acc[:, 0, :], c), start=True, stop=True).then_inc(s_m1, 1)
            for c in range(NCH):
                pe.wait_ge(s_silu, c + 1)
                pe.matmul(ps[c][:, 0:size(c)], mat(k, MATS["mw2"]), chunk(half, c), start=True, stop=True).then_inc(s_m2, 1)
            norm.tensor(pe)
            table.tensor(pe)

        @block.vector
        def _(dve):
            for c in range(NCH):
                dve.wait_ge(s_tanh, c + 1)
                dve.scalar_tensor_tensor(out=chunk(half, c), in0=chunk(t.sq, c), scalar=1.0, in1=chunk(half, c),
                                         op0=ALU.add, op1=ALU.mult).then_inc(s_silu, 1)
            for c in range(NCH):
                dve.wait_ge(s_m2, c + 1)
                dve.scalar_tensor_tensor(out=chunk(k.x, c), in0=ps[c][:, 0:size(c)], scalar=col(k, COLS["mb2"]), in1=chunk(k.x, c),
                                         op0=ALU.add, op1=ALU.add).then_inc(s_x1, 1)
                dve.wait_ge(s_x1, c + 1)
                dve.tensor_tensor(chunk(k.x, c), chunk(k.x, c), chunk(k.h, c), ALU.add).then_inc(s_x, 1)
            norm.vector(dve)
            table.vector(dve)


def nodes_after_mean(nc, k):
    with Tensors(nc, k, "n2") as t:
        ps = node_tensors(t)
        s_deg, s_log, s_rdeg, s_mean, s_alone, s_m, s_relu, s_x = (t.sem(n) for n in ("deg", "log", "rdeg", "mean", "alone", "m", "relu", "x"))
        s_hm, s_near, s_exact = t.sem("hm"), t.sem("near"), t.sem("exact")
        near = t.sb("near", [P, NP])
        norm = Norm(t, "norm", k, k.x, k.h, ps, s_x)
        table = Table(t, k, k.h, ps, norm.s_out, k.ident[:], None, [(k.dram["t128"], 0, P)])
        block = t.block()

        @block.sync
        def _(sp):
            table.sync(sp)

        @block.gpsimd
        def _(pool):
            for c in range(NCH):
                pool.tensor_scalar(chunk(t.sq, c), chunk(k.acc[:, 1, :], c), 1.0, None, ALU.max).then_inc(s_deg, 1)

        @block.scalar
        def _(act):
            for batch in (range(0, 2), range(2, 4), range(4, NCH)):
                for c in batch:
                    act.wait_ge(s_deg, c + 1)
                    act.activation(chunk(t.sq, c), chunk(t.sq, c), ACT.Ln).then_inc(s_log, 1)
                for c in batch:
                    inverse(act, t.sq, c, s_log, s_rdeg)
            for c in range(NCH):
                act.wait_ge(s_m, c + 1)
                act.activation(chunk(t.dev, c), ps[c][:, 0:size(c)], ACT.Relu, bias=col(k, COLS["L1"])).then_inc(s_relu, 1)
            norm.scalar(act)

        @block.tensor
        def _(pe):
            for c in range(NCH):
                pe.wait_ge(s_mean, c + 1)
                pe.matmul(ps[c][:, 0:size(c)], mat(k, MATS["L1"]), chunk(t.sq, c), start=True, stop=True).then_inc(s_m, 1)
            norm.tensor(pe)
            table.tensor(pe)

        @block.vector
        def _(dve):
            for c in range(NCH):
                total, deg = (chunk(k.acc[:, i, :], c) for i in range(2))
                dve.scalar_tensor_tensor(out=chunk(t.dev, c), in0=deg, scalar=0.0, in1=chunk(k.h, c),
                                         op0=ALU.is_equal, op1=ALU.mult).then_inc(s_alone, 1)
                dve.wait_ge(s_rdeg, c + 1)
                dve.scalar_tensor_tensor(out=chunk(near, c), in0=deg, scalar=1.0, in1=chunk(t.sq, c), op0=ALU.max, op1=ALU.mult).then_inc(s_near, 1)
                dve.wait_ge(s_near, c + 1)
                dve.scalar_tensor_tensor(out=chunk(t.sq, c), in0=chunk(near, c), scalar=2.0, in1=chunk(t.sq, c),
                                         op0=ALU.subtract, op1=ALU.mult).then_inc(s_exact, 1)
                dve.wait_ge(s_exact, c + 1)
                dve.tensor_tensor(chunk(t.sq, c), total, chunk(t.sq, c), ALU.mult).then_inc(s_hm, 1)
                dve.wait_ge(s_hm, c + 1)
                dve.wait_ge(s_alone, c + 1)
                dve.tensor_tensor(chunk(t.sq, c), chunk(t.dev, c), chunk(t.sq, c), ALU.subtract).then_inc(s_mean, 1)
            for c in range(NCH):
                dve.wait_ge(s_relu, c + 1)
                dve.tensor_tensor(chunk(k.x, c), chunk(k.x, c), chunk(t.dev, c), ALU.add).then_inc(s_x, 1)
            norm.vector(dve)
            table.vector(dve)


def layer_table(t, k, h, ps, ready, layer):
    a = (LAYER_ROWS + 4 * layer) * P
    return Table(t, k, h, ps, ready, mat(k, LAYER_MATS + 5 * layer, 3), k.rows[:, a:a + 3 * P],
                 [(k.dram["t256"], 0, 2 * P), (k.dram["t_dst"], 2 * P, 3 * P)], more=k.rows[:, a + 3 * P:a + 4 * P])


def nodes_after_sum(nc, k):
    with Tensors(nc, k, "n3") as t:
        ps = node_tensors(t)
        hid = t.sb("hid", [P, 2, CH])
        pre = k.acc[:, 1, :]
        s_hid, s_hidr, s_w2, s_pre1, s_pre, s_x, s_emb, s_h = (t.sem(n) for n in ("hid", "hidr", "w2", "pre1", "pre", "x", "emb", "h"))
        norm_out = Norm(t, "out", k, pre, t.dev, ps, s_pre, affine=True)
        norm = Norm(t, "norm", k, k.x, k.h, ps, s_x)
        table = layer_table(t, k, k.h, ps, s_h, 0)
        block = t.block()

        @block.sync
        def _(sp):
            table.sync(sp)

        @block.scalar
        def _(act):
            for n in range(4 * NCH):
                q = n % 4
                act.wait_ge(s_hid, n + 1)
                wait(act, s_w2, n - 1)
                act.activation(hid[:, n % 2, 0:size(n // 4)], ps[n % 2][:, 0:size(n // 4)], ACT.Relu, bias=col(k, COLS["b1"] + q)).then_inc(s_hidr, 1)
            norm_out.scalar(act)
            norm.scalar(act)
            for c in range(NCH):
                act.wait_ge(s_emb, c + 1)
                act.activation(chunk(k.h, c), ps[c][:, 0:size(c)], ACT.Identity, bias=col(k, COLS["emb_h"])).then_inc(s_h, 1)

        @block.tensor
        def _(pe):
            def up(n):
                c, q = n // 4, n % 4
                wait(pe, s_hidr, n - 1)
                pe.matmul(ps[n % 2][:, 0:size(c)], mat(k, MATS["W1"] + q), chunk(k.acc[:, 0, :], c), start=True, stop=True).then_inc(s_hid, 1)

            table.biases(pe)
            up(0)
            for n in range(4 * NCH):
                c, q = n // 4, n % 4
                if n + 1 < 4 * NCH:
                    up(n + 1)
                pe.wait_ge(s_hidr, n + 1)
                if q == 0:
                    wait(pe, s_pre1, c - 1)
                pe.matmul(ps[2 + c % 2][:, 0:size(c)], mat(k, MATS["W2"] + q), hid[:, n % 2, 0:size(c)], start=q == 0, stop=q == 3).then_inc(s_w2, 1)
            norm_out.tensor(pe)
            norm.tensor(pe)
            for c in range(NCH):
                pe.wait_ge(norm.s_out, c + 1)
                pe.matmul(ps[c][:, 0:size(c)], mat(k, MATS["emb_h"]), chunk(k.h, c), start=True, stop=True).then_inc(s_emb, 1)
            table.tensor(pe)

        @block.vector
        def _(dve):
            table.spread(dve)
            for c in range(NCH):
                dve.wait_ge(s_w2, 4 * c + 4)
                dve.scalar_tensor_tensor(out=chunk(pre, c), in0=ps[2 + c % 2][:, 0:size(c)], scalar=col(k, COLS["b2"]), in1=chunk(k.h, c),
                                         op0=ALU.add, op1=ALU.add).then_inc(s_pre1, 1)
            dve.wait_ge(s_pre1, NCH)
            dve.sem_inc(s_pre, NCH)
            norm_out.vector(dve)
            for c in range(NCH):
                dve.wait_ge(norm_out.s_out, c + 1)
                dve.tensor_tensor(chunk(k.x, c), chunk(k.x, c), chunk(t.dev, c), ALU.add).then_inc(s_x, 1)
            norm.vector(dve)
            table.vector(dve)


def nodes_after_gates(nc, k, layer):
    final = layer == LAYERS - 1
    with Tensors(nc, k, f"n{4 + layer}") as t:
        ps = node_tensors(t)
        stats = t.sb("node_stats", [P, NCH, 6])
        moments = t.sb("moments", [P, 2, 2])
        std = t.sb("std", [P, 2])
        scale_node = t.sb("scale_node", [P, 1])
        shift_node = t.sb("shift_node", [P, 1])
        s_a, s_log, s_rden, s_gate, s_new, s_stats, s_relu, s_h, s_out = (
            t.sem(n) for n in ("a", "log", "rden", "gate", "new", "stats", "relu", "h", "out"))
        s_mom, s_std, s_dve = t.sem("moments"), t.sem("std"), t.sem("dve_step")
        s_bn, s_eps, s_odd, s_even, s_exact, s_xh = (t.sem(n) for n in ("bn_terms", "eps", "odd", "even", "exact", "xh"))
        near = t.sb("near", [P, NP])
        if not final:
            table = layer_table(t, k, k.h, ps, s_h, layer + 1)
        c0 = LAYER_COLS + 5 * layer
        block = t.block()

        @block.sync
        def _(sp):
            if final:
                for c in range(NCH):
                    sp.wait_ge(s_h, c + 1)
                    n = LAST if c == NCH - 1 else CH
                    sp.dma_start(k.dram["out"][:, c * CH:c * CH + n], chunk(k.x, c, n)).then_inc(s_out, 16)
                sp.wait_ge(s_out, 16 * NCH)
            else:
                table.sync(sp)

        @block.gpsimd
        def _(pool):
            for c in range(1, NCH, 2):
                pool.tensor_scalar(chunk(near, c), chunk(k.acc[:, 1, :], c), GATE_EPS, None, ALU.add).then_inc(s_eps, 1)
            for n, c in enumerate(range(1, NCH, 2)):
                pool.wait_ge(s_eps, n + 1)
                pool.wait_ge(s_rden, c + 1)
                pool.tensor_tensor(chunk(near, c), chunk(near, c), chunk(t.sq, c), ALU.mult).then_inc(s_odd, 1)
            if final:
                for c in range(NCH):
                    pool.tensor_tensor(chunk(k.x, c), chunk(k.x, c), chunk(k.h, c), ALU.add).then_inc(s_xh, 1)

        @block.scalar
        def _(act):
            for batch in (range(0, 3), range(3, NCH)):
                for c in batch:
                    act.activation(chunk(t.sq, c), chunk(k.acc[:, 1, :], c), ACT.Ln, bias=k.gate_eps[:]).then_inc(s_log, 1)
                for c in batch:
                    inverse(act, t.sq, c, s_log, s_rden)
            act.wait_ge(s_mom, 1)
            act.activation(std[:], moments[:, :, 1], ACT.Sqrt, bias=k.ln_eps[:]).then_inc(s_std, 1)
            act.wait_ge(s_bn, 1)
            for c in range(NCH):
                act.activation(chunk(t.sq, c), chunk(t.dev, c), ACT.Relu, bias=shift_node[:], scale=scale_node[:]).then_inc(s_relu, 1)

        @block.tensor
        def _(pe):
            for c in range(NCH):
                pe.matmul(ps[c][:, 0:size(c)], mat(k, LAYER_MATS + 5 * layer + 3), chunk(k.h, c), start=True, stop=True).then_inc(s_a, 1)
            if not final:
                table.biases(pe)
                table.tensor(pe)

        @block.vector
        def _(dve):
            steps = [0]

            def then(instruction):
                steps[0] += 1
                instruction.then_inc(s_dve, 1)
                dve.wait_ge(s_dve, steps[0])

            for c in range(NCH):
                if c % 2:
                    dve.wait_ge(s_odd, c // 2 + 1)
                else:
                    dve.wait_ge(s_rden, c + 1)
                    dve.scalar_tensor_tensor(out=chunk(near, c), in0=chunk(k.acc[:, 1, :], c), scalar=GATE_EPS, in1=chunk(t.sq, c),
                                             op0=ALU.add, op1=ALU.mult).then_inc(s_even, 1)
                    dve.wait_ge(s_even, c // 2 + 1)
                dve.scalar_tensor_tensor(out=chunk(t.sq, c), in0=chunk(near, c), scalar=2.0, in1=chunk(t.sq, c),
                                         op0=ALU.subtract, op1=ALU.mult).then_inc(s_exact, 1)
                dve.wait_ge(s_exact, c + 1)
                dve.tensor_tensor(chunk(t.sq, c), chunk(k.acc[:, 0, :], c), chunk(t.sq, c), ALU.mult).then_inc(s_gate, 1)
                dve.wait_ge(s_gate, c + 1)
                dve.wait_ge(s_a, c + 1)
                dve.scalar_tensor_tensor(out=chunk(t.dev, c), in0=ps[c][:, 0:size(c)], scalar=col(k, c0), in1=chunk(t.sq, c),
                                         op0=ALU.add, op1=ALU.subtract).then_inc(s_new, 1)
                dve.wait_ge(s_new, c + 1)
                dve.bn_stats(stats[:, c, :], chunk(t.dev, c, LAST if c == NCH - 1 else None)).then_inc(s_stats, 1)
            dve.wait_ge(s_stats, NCH)
            then(dve.bn_aggr(moments[:, 0, :], stats[:].rearrange("p c s -> p (c s)")))
            if final:
                then(dve.tensor_copy(moments[:, 1, :], moments[:, 0, :]))
            else:
                then(dve.bn_aggr(moments[:, 1, :], k.stats[:]))
            dve.sem_inc(s_mom, 1)
            dve.wait_ge(s_std, 1)
            then(dve.reciprocal(std[:], std[:]))
            then(dve.tensor_tensor(scale_node[:], std[:, 0:1], col(k, c0 + 1), ALU.mult))
            then(dve.tensor_tensor(shift_node[:], moments[:, 0, 0:1], scale_node[:], ALU.mult))
            then(dve.tensor_tensor(shift_node[:], col(k, c0 + 2), shift_node[:], ALU.subtract))
            if not final:
                scale, shift = k.scale_edge[:, layer:layer + 1], k.shift_edge[:, layer:layer + 1]
                then(dve.tensor_tensor(scale, std[:, 1:2], col(k, c0 + 3), ALU.mult))
                then(dve.tensor_tensor(shift, moments[:, 1, 0:1], scale, ALU.mult))
                then(dve.tensor_tensor(shift, col(k, c0 + 4), shift, ALU.subtract))
            dve.sem_inc(s_bn, 1)
            if not final:
                table.spread(dve)
            for c in range(NCH):
                dve.wait_ge(s_relu, c + 1)
                if final:
                    dve.wait_ge(s_xh, c + 1)
                    dve.tensor_tensor(chunk(k.x, c), chunk(k.x, c), chunk(t.sq, c), ALU.add).then_inc(s_h, 1)
                else:
                    dve.tensor_tensor(chunk(k.h, c), chunk(k.h, c), chunk(t.sq, c), ALU.add).then_inc(s_h, 1)
            if not final:
                table.vector(dve)



def warm(pe, k, ps):
    for _ in range(WARM):
        pe.matmul(ps[:, 0:CH], mat(k, 0), k.mats[:, 0:CH], start=True, stop=True)


def rows_count(k, j):
    each = 16 * T * k.gathers
    return k.gathered_before + each + each * j.round


def gather_rows(pool, k, t, table, rows, idx, s_idx, s_seen, s_rows, s_free, table_dst=None, rows_by_dst=None, idx_dst=None, s_idx_dst=None):
    by_dst = rows_by_dst is not None

    def step(r, u):
        j = At(r, u)
        wait(pool, s_free, j.g - U + 1)
        pool.wait_ge(s_idx, j.g + 1)
        pool.sem_inc(s_seen, 1)
        if by_dst:
            pool.tensor_copy(idx_dst[:, u * T:(u + 1) * T], k.dst_idx[:, bass.ds(j.g * T, T)]).then_inc(s_idx_dst, 1)
            pool.wait_ge(s_idx_dst, j.g + 1)
            pool.sem_inc(s_seen, 1)
        for q in range(T):
            pool.indirect_dma_start(out=rows[:, u, q, :], out_offset=None, in_=table,
                                    in_offset=bass.IndirectOffsetOnAxis(ap=idx[:, u * T + q:u * T + q + 1], axis=0)).then_inc(s_rows[u], 16)
            if by_dst:
                pool.indirect_dma_start(out=rows_by_dst[:, u, q, :], out_offset=None, in_=table_dst,
                                        in_offset=bass.IndirectOffsetOnAxis(ap=idx_dst[:, u * T + q:u * T + q + 1], axis=0)).then_inc(s_rows[u], 16)

    groups(pool, step)


def next_idx(dve, k, idx, s_idx, j):
    if j.exists:
        dve.tensor_copy(idx[:, j.slot * T:(j.slot + 1) * T], k.src[:, bass.ds(j.g * T, T)]).then_inc(s_idx, 1)


def first_idx(dve, k, idx, s_idx):
    for u in range(U):
        next_idx(dve, k, idx, s_idx, At(0, u))


def window_of(dve, k, g):
    if k.general:
        return None
    return dve.value_load(k.window[0:1, bass.ds(g, 1)], min_val=0, max_val=NP - W)


class Scatter:

    def __init__(self, t, k, blocks, scaled=False):
        self.k, self.blocks, self.scaled = k, blocks, scaled
        self.onehot = t.sb("onehot", [P, U, T, W])
        self.ps = [t.ps(f"sum{i}") for i in range(2)]
        self.behind = 1 if k.general else 2
        self.s_zero = t.sem("zero")
        self.s_oh = t.sem("oh")
        self.s_sum = t.sem("sum")
        self.s_acc = t.sem("acc")
        self.s_enter = t.sem("enter")
        self.s_window = t.sem("window")

    def make(self, dve, out, j, iota):
        k = self.k
        if self.scaled:
            for q in range(T):
                last = dve.tensor_scalar(out[:, q, :], iota, k.place[:, q, bass.ds(j.g, 1)], k.cut[:, bass.ds(j.g * T + q, 1)],
                                         ALU.is_equal, ALU.mult)
        else:
            last = dve.tensor_tensor(out, k.place[:, :, bass.ds(j.g, 1)].broadcast_to([P, T, W]),
                                     iota.unsqueeze(1).broadcast_to([P, T, W]), ALU.is_equal)
        last.then_inc(self.s_oh, 1)

    def start(self, dve):
        dve.memset(self.k.acc[:], 0.0).then_inc(self.s_zero, 1)
        dve.wait_ge(self.s_zero, 1)
        if self.k.general:
            dve.sem_inc(self.s_acc, 1)

    def hot(self, dve, j):
        if j.exists and not self.k.general:
            wait(dve, self.s_sum, j.g - U + 1)
            self.make(dve, self.onehot[:, j.slot], j, self.k.iota[:])

    def products(self, pe, ps, slot, values):
        for a, tiles in enumerate(values):
            for n, (q, tile) in enumerate(tiles):
                last = pe.matmul(ps[:, a * W:(a + 1) * W], tile, self.onehot[:, slot, q, :], start=n == 0, stop=n == len(tiles) - 1)
        return last

    def tensor(self, pe, j, values):
        if not self.k.general:
            pe.wait_ge(self.s_oh, j.g + 1)
            wait(pe, self.s_acc, j.g - 1)
            self.products(pe, self.ps[j.two], j.slot, values).then_inc(self.s_sum, 1)
            return
        pe.sem_inc(self.s_enter, 1)
        with pe.Fori(0, NW) as w:
            pe.wait_ge(self.s_oh, j.g * NW + w + 1)
            pe.wait_ge(self.s_acc, j.g * NW + w + 1)
            self.products(pe, self.ps[0], 0, values).then_inc(self.s_window, 1)
        pe.wait_ge(self.s_window, (j.g + 1) * NW)
        pe.sem_inc(self.s_sum, 1)

    def add(self, dve, j):
        k, n = self.k, self.blocks
        if not j.exists:
            return
        if not k.general:
            window = window_of(dve, k, j.g)
            dve.wait_ge(self.s_sum, j.g + 1)
            wait(dve, self.s_acc, j.g)
            acc = k.acc[:, 0:n, bass.ds(window, W)]
            dve.tensor_tensor(acc, acc, self.ps[j.two][:, 0:n * W].rearrange("p (a w) -> p a w", a=n), ALU.add).then_inc(self.s_acc, 1)
            return
        dve.sem_inc(self.s_enter, 1)
        with dve.Fori(0, NW) as w:
            self.make(dve, self.onehot[:, 0], j, k.iota_all[:, bass.ds(w * W, W)])
            dve.wait_ge(self.s_window, j.g * NW + w + 1)
            dve.wait_ge(self.s_acc, j.g * NW + w + 1)
            acc = k.acc[:, 0:n, bass.ds(w * W, W)]
            dve.tensor_tensor(acc, acc, self.ps[0][:, 0:n * W].rearrange("p (a w) -> p a w", a=n), ALU.add).then_inc(self.s_acc, 1)


def edges_filter(nc, k):
    with Tensors(nc, k, "e0") as t:
        idx = t.sb("idx", [P, U * T], I32)
        rows = t.sb("rows", [P, U, T, P])
        dist = t.sb("dist", [RBF, U, GE])
        rbf = t.sb("rbf", [RBF, 2, GE])
        half = t.sb("half", [P, 2, GE])
        hid = t.sb("hid", [P, 2, GE])
        filt = t.sb("filt", [P, 2, T, P])
        ps_hid = [t.ps(f"hid{i}") for i in range(2)]
        ps_filt = [t.ps(f"filt{i}") for i in range(2)]
        scatter = Scatter(t, k, 1, scaled=True)
        s_idx, s_seen = t.sem("idx"), t.sem("seen")
        s_rows, s_dist = k.gathered, t.sems("dist", U)
        s_sq, s_rbf, s_up, s_half, s_tanh, s_hid, s_down, s_biased, s_msg = (
            t.sem(n) for n in ("sq", "rbf", "up", "half", "tanh", "hid", "down", "biased", "msg"))
        block = t.block()

        @block.gpsimd
        def _(pool):
            gather_rows(pool, k, t, k.dram["t128"], rows, idx, s_idx, s_seen, s_rows, s_msg)

        @block.sync
        def _(sp):
            def step(r, u):
                j = At(r, u)
                wait(sp, s_sq, j.g - U + 1)
                sp.dma_start(dist[:, u, :], k.dram["dist_row"][:, bass.ds(j.g * GE, GE)].broadcast_to([RBF, GE])).then_inc(s_dist[u], 16)

            groups(sp, step)

        @block.scalar
        def _(act):
            def basis(j):
                if not j.exists:
                    return
                act.wait_ge(s_dist[j.slot], 16 * (j.round + 1))
                wait(act, s_up, j.g - 1)
                act.activation(rbf[:, j.two, :], dist[:, j.slot, :], ACT.Square, bias=k.minus_centre[0:RBF, :]).then_inc(s_sq, 1)
                act.wait_ge(s_sq, j.g + 1)
                act.activation(rbf[:, j.two, :], rbf[:, j.two, :], ACT.Exp, scale=-1.0 / (2.0 * WIDTH * WIDTH)).then_inc(s_rbf, 1)

            def halves(j):
                if not j.exists:
                    return
                act.wait_ge(s_up, j.g + 1)
                wait(act, s_hid, j.g - 1)
                act.activation(half[:, j.two, :], ps_hid[j.two][:], ACT.Identity, bias=col(k, COLS["half_fb1"]), scale=0.5).then_inc(s_half, 1)
                act.wait_ge(s_half, j.g + 1)
                wait(act, s_down, j.g - 1)
                act.activation(hid[:, j.two, :], half[:, j.two, :], ACT.Tanh).then_inc(s_tanh, 1)

            basis(At(0, 0))
            basis(At(0, 1))
            halves(At(0, 0))
            basis(At(0, 2))
            halves(At(0, 1))

            def step(r, u):
                basis(At(r, u, 3))
                halves(At(r, u, 2))

            groups(act, step)

        @block.tensor
        def _(pe):
            def up(j):
                if not j.exists:
                    return
                pe.wait_ge(s_rbf, j.g + 1)
                wait(pe, s_half, j.g - 1)
                pe.matmul(ps_hid[j.two][:], k.fw1[:], rbf[:, j.two, :], start=True, stop=True).then_inc(s_up, 1)

            def down(j):
                if not j.exists:
                    return
                pe.wait_ge(s_hid, j.g + 1)
                wait(pe, s_biased, j.g - 1)
                for q in range(T):
                    last = pe.matmul(ps_filt[j.two][:, q * P:(q + 1) * P], hid[:, j.two, q * P:(q + 1) * P], mat(k, MATS["fw2"]), start=True, stop=True)
                last.then_inc(s_down, 1)

            def sums(j):
                if not j.exists:
                    return
                pe.wait_ge(s_msg, j.g + 1)
                scatter.tensor(pe, j, [[(q, filt[:, j.two, q, :]) for q in range(T)]])

            warm(pe, k, ps_filt[0])
            up(At(0, 0))
            up(At(0, 1))
            down(At(0, 0))
            up(At(0, 2))
            down(At(0, 1))

            def step(r, u):
                sums(At(r, u, -1))
                up(At(r, u, 3))
                down(At(r, u, 2))

            groups(pe, step)
            sums(At(R - 1, U - 1))

        @block.vector
        def _(dve):
            def hidden(j):
                if not j.exists:
                    return
                dve.wait_ge(s_tanh, j.g + 1)
                dve.scalar_tensor_tensor(out=hid[:, j.two, :], in0=hid[:, j.two, :], scalar=1.0, in1=half[:, j.two, :],
                                         op0=ALU.add, op1=ALU.mult).then_inc(s_hid, 1)

            def step(r, u):
                j = At(r, u)
                hidden(At(r, u, 2))
                scatter.hot(dve, At(r, u, 1))
                dve.wait_ge(s_down, j.g + 1)
                wait(dve, scatter.s_sum, j.g - 1)
                dve.tensor_tensor(filt[:, j.two], ps_filt[j.two][:].rearrange("p (q f) -> p q f", q=T),
                                  k.fb2[:].unsqueeze(1).broadcast_to([P, T, P]), ALU.add).then_inc(s_biased, 1)
                dve.wait_ge(s_biased, j.g + 1)
                dve.wait_ge(s_rows[u], rows_count(k, j))
                dve.tensor_tensor(filt[:, j.two], filt[:, j.two], rows[:, u], ALU.mult).then_inc(s_msg, 1)
                next_idx(dve, k, idx, s_idx, At(r, u, U))
                scatter.add(dve, At(r, u, -scatter.behind))

            first_idx(dve, k, idx, s_idx)
            scatter.start(dve)
            scatter.hot(dve, At(0, 0))
            hidden(At(0, 0))
            hidden(At(0, 1))
            groups(dve, step)
            for u in range(U - scatter.behind, U):
                scatter.add(dve, At(R - 1, u))


def edges_sum(nc, k, with_edges):
    with Tensors(nc, k, "e2" if with_edges else "e1") as t:
        idx = t.sb("idx", [P, U * T], I32)
        rows = t.sb("rows", [P, U, T, P])
        edge = t.sb("edge", [P, U, T, P]) if with_edges else None
        attr_t = None if with_edges else t.sb("attr_t", [P, U, GE])
        e0 = None if with_edges else t.sb("e0", [P, U, GE])
        ps_emb = [] if with_edges else [t.ps(f"emb{i}") for i in range(2)]
        scatter = Scatter(t, k, 1 if with_edges else 2)
        s_idx, s_seen, s_emb, s_e = t.sem("idx"), t.sem("seen"), t.sem("emb"), t.sem("e")
        s_rows, s_edge, s_keep = k.gathered, t.sems("edge", U), t.sems("keep", U)
        block = t.block()

        @block.gpsimd
        def _(pool):
            gather_rows(pool, k, t, k.dram["t128"], rows, idx, s_idx, s_seen, s_rows, scatter.s_sum)

        if with_edges:
            @block.sync
            def _(sp):
                def step(r, u):
                    j = At(r, u)
                    wait(sp, scatter.s_sum, j.g - U + 1)
                    sp.dma_start(edge[:, u], k.dram["attr"][bass.ds(j.g * GE, GE), :].rearrange("(q p) f -> p q f", p=P)).then_inc(s_edge[u], 16)

                groups(sp, step)
        else:
            @block.sync
            def _(sp):
                def load(j):
                    if not j.exists:
                        return
                    wait(sp, s_emb, j.g - U + 1)
                    sp.dma_start(attr_t[:, j.slot, :], k.dram["attr_t"][:, bass.ds(j.g * GE, GE)]).then_inc(s_edge[j.slot], 16)

                for u in range(U):
                    load(At(0, u))

                def step(r, u):
                    j = At(r, u)
                    load(At(r, u, U))
                    sp.wait_ge(s_e, j.g + 1)
                    sp.dma_start(k.dram["e0"][:, bass.ds(j.g * GE, GE)], e0[:, u, :]).then_inc(s_keep[u], 16)

                groups(sp, step)
                for u in range(U):
                    sp.wait_ge(s_keep[u], 16 * R)

            @block.scalar
            def _(act):
                def step(r, u):
                    j = At(r, u)
                    act.wait_ge(s_emb, j.g + 1)
                    wait(act, s_keep[u], 16 * j.round)
                    act.activation(e0[:, u, :], ps_emb[j.two][:], ACT.Identity, bias=col(k, COLS["emb_e"])).then_inc(s_e, 1)

                groups(act, step)

        @block.tensor
        def _(pe):
            def step(r, u):
                j = At(r, u)
                if not with_edges:
                    pe.wait_ge(s_edge[u], 16 * (j.round + 1))
                    wait(pe, s_e, j.g - 1)
                    pe.matmul(ps_emb[j.two][:], mat(k, MATS["emb_e"]), attr_t[:, u, :], start=True, stop=True).then_inc(s_emb, 1)
                pe.wait_ge(s_rows[u], rows_count(k, j))
                by_src = [(q, rows[:, u, q, :]) for q in range(T)]
                if with_edges:
                    pe.wait_ge(s_edge[u], 16 * (j.round + 1))
                    scatter.tensor(pe, j, [by_src + [(q, edge[:, u, q, :]) for q in range(T)]])
                else:
                    scatter.tensor(pe, j, [by_src, [(q, k.ones[:]) for q in range(T)]])

            groups(pe, step)

        @block.vector
        def _(dve):
            def step(r, u):
                scatter.hot(dve, At(r, u, 1))
                scatter.add(dve, At(r, u))
                next_idx(dve, k, idx, s_idx, At(r, u, U))

            first_idx(dve, k, idx, s_idx)
            scatter.start(dve)
            scatter.hot(dve, At(0, 0))
            groups(dve, step)


def edges_gates(nc, k, layer):
    final = layer == LAYERS - 1
    keeps = layer == 1
    since = [[], [0], [1], [1, 2]][layer]
    with Tensors(nc, k, f"g{layer}") as t:
        idx = t.sb("idx", [P, U * T], I32)
        rows = t.sb("rows", [P, U, T, 2 * P])
        dst_rows = t.sb("dst_rows", [W, U, P])
        e_in = t.sb("e_in", [P, U, GE])
        new_in = [t.sb(f"new_in{l}", [P, U, GE]) for l in since]
        relu = [t.sb(f"relu{l}", [P, 2, GE]) for l in since]
        e = t.sb("e", [P, U, GE]) if since else e_in
        rows_by_dst = t.sb("rows_by_dst", [P, U, T, P]) if k.general else None
        idx_dst = t.sb("idx_dst", [P, U * T], I32) if k.general else None
        scatter = Scatter(t, k, 2)
        onehot_t = t.sb("onehot_t", [W, 2, GE])
        new = t.sb("new", [P, 2, T, P])
        sig = t.sb("sig", [P, 2, T, P])
        gated = t.sb("gated", [P, 2, T, P])
        new_t = None if final else t.sb("new_t", [P, U, GE])
        stat4 = t.sb("stat4", [P, U, 6])
        ps_new = [t.ps(f"new{i}") for i in range(2)]
        ps_t = [t.ps(f"t{i}") for i in range(2)]
        ps_oh = t.ps("oh")
        s_idx, s_seen, s_turning, s_by_src, s_idx_dst = t.sem("idx"), t.sem("seen"), t.sem("turning"), t.sem("by_src"), t.sem("idx_dst")
        s_rows, s_load = k.gathered, t.sems("load", U)
        s_keep_e, s_keep_new = t.sems("keep_e", U), t.sems("keep_new", U)
        s_turn, s_oht, s_relu, s_first, s_e, s_ce, s_new, s_sig, s_gated, s_t, s_newt, s_bn, s_stat = (
            t.sem(n) for n in ("turn", "oht", "relu", "first", "e", "ce", "new", "sig", "gated", "t", "newt", "bn", "stat"))
        loads = 1 + len(since) + (not k.general)
        e_from = k.dram["e0" if layer < 2 else "e1"]
        wC = mat(k, LAYER_MATS + 5 * layer + 4)
        block = t.block()

        @block.gpsimd
        def _(pool):
            gather_rows(pool, k, t, k.dram["t256"], rows, idx, s_idx, s_seen, s_rows, s_gated, k.dram["t_dst"], rows_by_dst, idx_dst, s_idx_dst)

        @block.sync
        def _(sp):
            def load(j):
                if not j.exists:
                    return
                window = window_of(sp, k, j.g)
                wait(sp, s_ce, j.g - U + 1)
                sp.dma_start(e_in[:, j.slot, :], e_from[:, bass.ds(j.g * GE, GE)]).then_inc(s_load[j.slot], 16)
                for l, values in zip(since, new_in):
                    sp.dma_start(values[:, j.slot, :], k.dram[f"new{l}"][:, bass.ds(j.g * GE, GE)]).then_inc(s_load[j.slot], 16)
                if not k.general:
                    sp.dma_start(dst_rows[:, j.slot, :], k.dram["t_dst"][bass.ds(window, W), :]).then_inc(s_load[j.slot], 16)

            for u in range(U):
                load(At(0, u))

            def step(r, u):
                j = At(r, u)
                load(At(r, u, U))
                if keeps:
                    sp.wait_ge(s_e, j.g + 1)
                    sp.dma_start(k.dram["e1"][:, bass.ds(j.g * GE, GE)], e[:, u, :]).then_inc(s_keep_e[u], 16)
                if not final:
                    sp.wait_ge(s_newt, j.g + 1)
                    sp.dma_start(k.dram[f"new{layer}"][:, bass.ds(j.g * GE, GE)], new_t[:, u, :]).then_inc(s_keep_new[u], 16)

            groups(sp, step)
            for u in range(U):
                if keeps:
                    sp.wait_ge(s_keep_e[u], 16 * R)
                if not final:
                    sp.wait_ge(s_keep_new[u], 16 * R)

        @block.scalar
        def _(act):
            def relu_of(j):
                if not j.exists or not since:
                    return
                act.wait_ge(s_load[j.slot], 16 * loads * (j.round + 1))
                wait(act, s_e, j.g - 1)
                for l, values, out in zip(since, new_in, relu):
                    last = act.activation(out[:, j.two, :], values[:, j.slot, :], ACT.Relu, bias=k.shift_edge[:, l:l + 1], scale=k.scale_edge[:, l:l + 1])
                last.then_inc(s_relu, 1)

            def turned(j):
                if not j.exists or k.general:
                    return
                act.wait_ge(s_turn, j.g + 1)
                wait(act, s_ce, j.g - 1)
                act.activation(onehot_t[:, j.two, :], ps_oh[0:W, :], ACT.Copy).then_inc(s_oht, 1)

            relu_of(At(0, 0))
            turned(At(0, 0))
            relu_of(At(0, 1))
            turned(At(0, 1))
            relu_of(At(0, 2))

            def step(r, u):
                j = At(r, u)
                act.wait_ge(s_new, j.g + 1)
                wait(act, scatter.s_sum, j.g - 1)
                act.activation(sig[:, j.two], new[:, j.two], ACT.Sigmoid).then_inc(s_sig, 1)
                relu_of(At(r, u, 3))
                if not final:
                    act.wait_ge(s_t, j.g + 1)
                    wait(act, s_keep_new[u], 16 * j.round)
                    wait(act, s_bn, j.g - U + 1)
                    act.activation(new_t[:, u, :], ps_t[j.two][:], ACT.Copy).then_inc(s_newt, 1)
                turned(At(r, u, 2))

            groups(act, step)

        @block.tensor
        def _(pe):
            def turn(j):
                if not j.exists or k.general:
                    return
                pe.wait_ge(scatter.s_oh, j.g + 1)
                wait(pe, s_oht, j.g)
                pe.sem_inc(s_turning, 1)
                for q in range(T):
                    last = pe.transpose(ps_oh[0:W, q * P:(q + 1) * P], scatter.onehot[:, j.slot, q, :], k.ident[:])
                last.then_inc(s_turn, 1)

            def edge_terms(j):
                if not j.exists:
                    return
                if not k.general:
                    pe.wait_ge(s_oht, j.g + 1)
                pe.wait_ge(s_load[j.slot], 16 * loads * (j.round + 1))
                if since:
                    pe.wait_ge(s_e, j.g + 1)
                wait(pe, s_new, j.g - 1)
                for q in range(T):
                    cols = ps_new[j.two][:, q * P:(q + 1) * P]
                    if not k.general:
                        pe.matmul(cols, onehot_t[:, j.two, q * P:(q + 1) * P], dst_rows[:, j.slot, :], start=True, stop=False)
                    last = pe.matmul(cols, e[:, j.slot, q * P:(q + 1) * P], wC, start=k.general, stop=True)
                last.then_inc(s_ce, 1)

            def sums(j):
                if not j.exists:
                    return
                pe.wait_ge(s_gated, j.g + 1)
                scatter.tensor(pe, j, [[(q, values[:, j.two, q, :]) for q in range(T)] for values in (gated, sig)])

            turn(At(0, 0))
            turn(At(0, 1))
            edge_terms(At(0, 0))

            def step(r, u):
                j = At(r, u)
                edge_terms(At(r, u, 1))
                if not final:
                    pe.wait_ge(s_new, j.g + 1)
                    wait(pe, s_newt, j.g - 1)
                    for q in range(T):
                        last = pe.transpose(ps_t[j.two][:, q * P:(q + 1) * P], new[:, j.two, q, :], k.ident[:])
                    last.then_inc(s_t, 1)
                turn(At(r, u, 2))
                sums(At(r, u, -1))

            groups(pe, step)
            sums(At(R - 1, U - 1))

        @block.vector
        def _(dve):
            def edge(j):
                if not j.exists or not since:
                    return
                dve.wait_ge(s_relu, j.g + 1)
                if keeps:
                    wait(dve, s_keep_e[j.slot], 16 * j.round)
                wait(dve, s_ce, j.g - U + 1)
                dve.wait_ge(s_load[j.slot], 16 * loads * (j.round + 1))
                out = e[:, j.slot, :]
                last = dve.tensor_tensor(out, e_in[:, j.slot, :], relu[0][:, j.two, :], ALU.add)
                if len(since) == 2:
                    last.then_inc(s_first, 1)
                    dve.wait_ge(s_first, j.g + 1)
                    last = dve.tensor_tensor(out, out, relu[1][:, j.two, :], ALU.add)
                last.then_inc(s_e, 1)

            first_idx(dve, k, idx, s_idx)
            scatter.start(dve)
            scatter.hot(dve, At(0, 0))
            scatter.hot(dve, At(0, 1))
            edge(At(0, 0))
            edge(At(0, 1))

            def counted(j):
                if final or not j.exists:
                    return
                dve.wait_ge(s_newt, j.g + 1)
                wait(dve, s_stat, j.round)
                dve.bn_stats(stat4[:, j.slot, :], new_t[:, j.slot, 0:ELAST if j.last else GE]).then_inc(s_bn, 1)
                if j.slot == U - 1:
                    dve.wait_ge(s_bn, j.g + 1)
                    dve.tensor_scalar(k.stats[:, bass.ds(j.round * U * 6, U * 6)], stat4[:].rearrange("p u s -> p (u s)"), 1.0, None,
                                      ALU.mult).then_inc(s_stat, 1)

            def step(r, u):
                j = At(r, u)
                scatter.hot(dve, At(r, u, 2))
                dve.wait_ge(s_ce, j.g + 1)
                dve.wait_ge(s_rows[u], rows_count(k, j))
                edge_terms = ps_new[j.two][:].rearrange("p (q f) -> p q f", q=T)
                if k.general:
                    dve.tensor_tensor(new[:, j.two], edge_terms, rows[:, u, :, 0:P], ALU.add).then_inc(s_by_src, 1)
                    dve.wait_ge(s_by_src, j.g + 1)
                    dve.tensor_tensor(new[:, j.two], new[:, j.two], rows_by_dst[:, u], ALU.add).then_inc(s_new, 1)
                else:
                    dve.tensor_tensor(new[:, j.two], edge_terms, rows[:, u, :, 0:P], ALU.add).then_inc(s_new, 1)
                edge(At(r, u, 2))
                dve.wait_ge(s_sig, j.g + 1)
                wait(dve, scatter.s_sum, j.g - 1)
                dve.tensor_tensor(gated[:, j.two], sig[:, j.two], rows[:, u, :, P:2 * P], ALU.mult).then_inc(s_gated, 1)
                next_idx(dve, k, idx, s_idx, At(r, u, U))
                counted(At(r, u, -1))
                scatter.add(dve, At(r, u, -scatter.behind))

            groups(dve, step)
            counted(At(R - 1, U - 1))
            for u in range(U - scatter.behind, U):
                scatter.add(dve, At(R - 1, u))


def all_windows(nc, k):
    with Tensors(nc, k, "all_windows") as t:
        iota_i = t.sb("iota_i", [P, NP], I32)
        dsti = t.sb("dsti", [P, G * T], I32)
        dstf = t.sb("dstf", [P, G * T])
        s_iota, s_dst, s_float, s_clamped = (t.sem(n) for n in ("iota", "dst", "float", "clamped"))
        block = t.block()

        @block.gpsimd
        def _(pool):
            pool.iota(iota_i[:], pattern=[[1, NP]], base=0, channel_multiplier=0).then_inc(s_iota, 1)

        @block.sync
        def _(sp):
            sp.dma_start(dsti[:], k.dram["dst"]).then_inc(s_dst, 16)

        @block.vector
        def _(dve):
            dve.wait_ge(s_iota, 1)
            dve.tensor_copy(k.iota_all[:], iota_i[:])
            dve.wait_ge(s_dst, 16)
            dve.tensor_copy(dstf[:], dsti[:]).then_inc(s_float, 1)
            dve.wait_ge(s_float, 1)
            dve.tensor_copy(k.place[:], dstf[:].rearrange("p (g q) -> p q g", q=T)).then_inc(s_float, 1)
            dve.wait_ge(s_float, 2)
            dve.tensor_scalar(dstf[:], dstf[:], 0.0, None, ALU.max).then_inc(s_clamped, 1)
            dve.wait_ge(s_clamped, 1)
            dve.tensor_copy(k.dst_idx[:], dstf[:])


def layers(nc, k, general):
    k.general, k.gathers, k.gathered_before = general, 1, 0
    k.path = "_any" if general else "_in"
    with Tensors(nc, k, "tables") as t:
        if general:
            k.iota_all = t.sb("iota_all", [P, NP])
            k.dst_idx = t.sb("dst_idx", [P, G * T], I32)
            all_windows(nc, k)
        nodes_first(nc, k)
        edges_filter(nc, k)
        gathered(k)
        nodes_after_filter(nc, k)
        edges_sum(nc, k, False)
        gathered(k)
        nodes_after_mean(nc, k)
        edges_sum(nc, k, True)
        gathered(k)
        nodes_after_sum(nc, k)
        k.gathers = 2 if general else 1
        for layer in range(LAYERS):
            edges_gates(nc, k, layer)
            gathered(k)
            nodes_after_gates(nc, k, layer)


def gathered(k):
    k.gathered_before += 16 * T * k.gathers * R


def program(nc, dram):
    k = Chip()
    k.dram = dram
    k.path = ""
    with Tensors(nc, k, "all") as t:
        k.gathered = [t.enter_context(nc.semaphore(f"gathered{u}")) for u in range(U)]
        k.mats = t.sb("mats", [P, NMATS * P])
        k.cols = t.sb("cols", [P, NCOLS])
        k.rows = t.sb("bias_rows", [1, NROWS * P])
        k.fw1 = t.sb("fw1", [RBF, P])
        k.x = t.sb("x", [P, NP])
        k.h = t.sb("h", [P, NP])
        k.acc = t.sb("acc", [P, 2, NP])
        k.src = t.sb("src", [P, G * T], I32)
        k.window = t.sb("window", [1, G], I32)
        k.missed = t.sb("missed", [1, 1], I32)
        k.place = t.sb("place", [P, T, G])
        k.cut = t.sb("cut", [P, G * T])
        k.iota = t.sb("iota", [P, W])
        k.ident = t.sb("ident", [P, P])
        k.ones = t.sb("ones", [P, P])
        k.mean_of = t.sb("mean_of", [P, P])
        k.ln_eps = t.sb("ln_eps", [P, 1])
        k.gate_eps = t.sb("gate_eps", [P, 1])
        k.minus_centre = t.sb("minus_centre", [P, 1])
        k.fb2 = t.sb("fb2", [P, P])
        k.stats = t.sb("stats", [P, G * 6])
        k.scale_edge = t.sb("scale_edge", [P, LAYERS - 1])
        k.shift_edge = t.sb("shift_edge", [P, LAYERS - 1])
        prepare(nc, k)
        missed = nc.values_load(k.missed[0:1, 0:1], min_val=0, max_val=P)
        with nc.If(missed == 0):
            layers(nc, k, False)
        with nc.Else():
            layers(nc, k, True)


def kernel(**inputs):
    import concourse.bacc as _bacc
    from concourse import mybir as _mybir
    from concourse.bass_utils import run_bass_kernel_spmd as _run

    a = {n: np.asarray(v) for n, v in inputs.items()}

    def tiles(v, fill):
        padded = np.full(EP, fill, v.dtype)
        padded[:E] = v
        return padded

    def column(v):
        return v.reshape(-1, P).T

    attr = np.zeros((EP, P), a["edge_attr_128"].dtype)
    attr[:E] = a["edge_attr_128"]
    x = np.zeros((P, NP), a["x"].dtype)
    x[:, :N] = a["x"].T
    src, dst, dist = tiles(a["src"], 0), tiles(a["dst"], -1), tiles(a["edge_weight"], 0)
    mats = [a["L0_gnn_fw2"], a["L0_gnn_pw"], a["L0_gnn_mw1"], a["L0_gnn_mw2"], a["L1_gnn_W"], a["L2_gnn_W1"]]
    mats += [a["L2_gnn_W2"][q * P:(q + 1) * P] for q in range(4)] + [a["L3_gnn_W_emb_h"], a["L3_gnn_W_emb_e"]]
    mats += [a[f"L3_gnn_{m}w"][layer] for layer in range(LAYERS) for m in "DBEAC"]
    cols = [a["L0_gnn_fb1"], a["L0_gnn_mb1"], a["L0_gnn_mb2"], a["L1_gnn_b"], a["L2_gnn_b1"], a["L2_gnn_b2"], a["L2_gnn_gamma"],
            a["L2_gnn_beta"], a["L3_gnn_b_emb_h"], a["L3_gnn_b_emb_e"], np.zeros(2 * P, np.float32)]
    cols += [a[f"L3_gnn_{m}"][layer] for layer in range(LAYERS) for m in ("Ab", "gh", "bh", "ge", "be")]
    rows = [a["L0_gnn_pb"], a["L0_gnn_fb2"]] + [a[f"L3_gnn_{m}b"][layer] for layer in range(LAYERS) for m in "DBEC"]
    arrays = {
        "x": x,
        "src": src.reshape(-1, P).T,
        "dst": dst.reshape(-1, P).T,
        "dst_first": dst.reshape(1, G, GE)[:, :, 0],
        "dist": dist.reshape(-1, P).T,
        "dist_row": dist.reshape(1, EP),
        "attr": attr,
        "attr_t": attr.T,
        "fw1": a["L0_gnn_fw1"],
        "mats": np.concatenate(mats, axis=1),
        "cols": np.concatenate([column(c) for c in cols], axis=1),
        "rows": np.concatenate(rows).reshape(1, -1),
    }
    arrays = {f"in_{n}": np.ascontiguousarray(v) for n, v in arrays.items()}
    nc = _bacc.Bacc("TRN2", target_bir_lowering=False, num_devices=1)
    dram = {n[3:]: nc.dram_tensor(n, v.shape, _mybir.dt.from_np(v.dtype), kind="ExternalInput").ap() for n, v in arrays.items()}
    scratch = {"t128": (NP, P), "t256": (NP, 2 * P), "t_dst": (NP, P), "e0": (P, EP), "e1": (P, EP), "new0": (P, EP), "new1": (P, EP), "new2": (P, EP)}
    for n, shape in scratch.items():
        dram[n] = nc.dram_tensor(n, shape, _mybir.dt.float32).ap()
    dram["out"] = nc.dram_tensor("out_x", (P, N), _mybir.dt.float32, kind="ExternalOutput").ap()
    program(nc, dram)
    result = _run(nc, [arrays], core_ids=[0])
    return np.ascontiguousarray(result.results[0]["out_x"].T)
```
